# Optimizing a Trainium2 kernel written in Bass

```python
import numpy as np
import jax
import jax.numpy as jnp

def _softmax(x, axis=-1):
    return jax.nn.softmax(x, axis=axis)

def _gelu(x):
    return jax.nn.gelu(x, approximate=True)

def _silu(x):
    return jax.nn.silu(x)

def _sigmoid(x):
    return jax.nn.sigmoid(x)

def _layernorm(x, axis=-1, eps=1e-05):
    m = jnp.mean(x, axis=axis, keepdims=True)
    v = jnp.var(x, axis=axis, keepdims=True)
    return (x - m) / jnp.sqrt(v + eps)

def _scatter_add(tgt, idx, src, axis=0):
    return tgt.at[idx].add(src)

def _segment_sum(src, seg, n):
    return jax.ops.segment_sum(src, seg, n)
kernel_name = 'mk_conv_seq_d2_conv_nchw384_r4_236d52'

def setup_inputs(seed: int=0):
    np.random.seed(seed)
    _w = jnp.asarray

    def _rec_inputs():
        import jax
        import jax.numpy as jnp
        _gk = jax.random.key(seed)
        x = -4.65e-05 + 0.9999 * jax.random.normal(jax.random.fold_in(_gk, 1), (32, 96, 16, 16), jnp.float32)
        return x
    x = _rec_inputs()

    def _L0_conv_setup():
        import jax, jax.numpy as jnp
        import numpy as np
        DIM = 96
        HEADS = 12
        WS = 8
        SS = 4
        N = WS * WS
        HEAD_DIM = DIM // HEADS
        SCALE = HEAD_DIM ** (-0.5)
        MLP_HID = int(DIM * 4.0)

        def _relative_position_index():
            ch, cw = np.meshgrid(np.arange(WS), np.arange(WS), indexing='ij')
            coords = np.stack([ch, cw]).reshape(2, -1)
            rel = coords[:, :, None] - coords[:, None, :]
            rel = rel.transpose(1, 2, 0).astype(np.int64)
            rel[:, :, 0] += WS - 1
            rel[:, :, 1] += WS - 1
            rel[:, :, 0] *= 2 * WS - 1
            return jnp.asarray(rel.sum(-1))
        REL_IDX = _relative_position_index()

        def _shift_mask(H, W):
            img = np.zeros((H, W), dtype=np.float32)
            slices = (slice(0, -WS), slice(-WS, -SS), slice(-SS, None))
            cnt = 0
            for hs in slices:
                for ws_ in slices:
                    img[hs, ws_] = cnt
                    cnt += 1
            mw = img.reshape(H // WS, WS, W // WS, WS).transpose(0, 2, 1, 3).reshape(-1, N)
            diff = mw[:, None, :] - mw[:, :, None]
            return jnp.asarray(np.where(diff != 0, -10.0, 0.0).astype(np.float32))

        def _layernorm(x, g, b, eps=1e-05):
            mu = x.mean(-1, keepdims=True)
            var = ((x - mu) ** 2).mean(-1, keepdims=True)
            return (x - mu) * jax.lax.rsqrt(var + eps) * g + b
        key = jax.random.key(seed)
        ks = jax.random.split(key, 16)
        s = lambda fan_in: 1.0 / np.sqrt(fan_in)
        return {'x': jax.random.normal(ks[0], (32, DIM, 16, 16), jnp.float32), 'qkv_w': jax.random.normal(ks[1], (DIM, 3 * DIM), jnp.float32) * s(DIM), 'qkv_b': jnp.zeros((3 * DIM,), jnp.float32), 'proj_w': jax.random.normal(ks[2], (DIM, DIM), jnp.float32) * s(DIM), 'proj_b': jnp.zeros((DIM,), jnp.float32), 'rel_bias': jax.random.normal(ks[3], ((2 * WS - 1) ** 2, HEADS), jnp.float32) * 0.02, 'norm1_g': jnp.ones((DIM,), jnp.float32), 'norm1_b': jnp.zeros((DIM,), jnp.float32), 'norm2_g': jnp.ones((DIM,), jnp.float32), 'norm2_b': jnp.zeros((DIM,), jnp.float32), 'fc1_w': jax.random.normal(ks[4], (DIM, MLP_HID), jnp.float32) * s(DIM), 'fc1_b': jnp.zeros((MLP_HID,), jnp.float32), 'fc2_w': jax.random.normal(ks[5], (MLP_HID, DIM), jnp.float32) * s(MLP_HID), 'fc2_b': jnp.zeros((DIM,), jnp.float32)}
    _L0_conv_all = _L0_conv_setup()
    _L0_conv_in = {k: v for k, v in _L0_conv_all.items() if k in ('qkv_w', 'qkv_b', 'proj_w', 'proj_b', 'rel_bias', 'norm1_g', 'norm1_b', 'norm2_g', 'norm2_b', 'fc1_w', 'fc1_b', 'fc2_w', 'fc2_b')}
    del _L0_conv_all

    def _L1_conv_setup():
        import jax, jax.numpy as jnp
        import numpy as np
        B, C, S, NH = (16, 96, 16, 8)
        HC = C // NH
        EPS = 1e-05

        def _dwconv(x, w, b):
            y = jax.lax.conv_general_dilated(x, w, window_strides=(1, 1), padding='SAME', feature_group_count=x.shape[1], dimension_numbers=('NCHW', 'OIHW', 'NCHW'))
            return y + b[None, :, None, None]

        def _proj(xn, wp, bp, wd, bd):
            b_, c_, s1, s2 = xn.shape
            xh = xn.reshape(b_, NH, HC, s1, s2)
            y = jnp.einsum('bhcij,hoc->bhoij', xh, wp) + bp[None, :, :, None, None]
            y = _dwconv(y.reshape(b_, c_, s1, s2), wd, bd).reshape(b_, NH, HC, s1, s2)
            return jnp.transpose(y, (0, 1, 4, 3, 2)).reshape(b_, NH, s2 * s1, HC)
        key = jax.random.key(seed)
        ks = jax.random.split(key, 10)
        sc = 0.05
        n = lambda k, shape: jax.random.normal(k, shape, jnp.float32) * sc
        return {'x': jax.random.normal(ks[0], (B, C, S, S), jnp.float32), 'ln_g': jnp.ones((C, S, S), jnp.float32), 'ln_b': jnp.zeros((C, S, S), jnp.float32), 'wq_p': n(ks[1], (NH, HC, HC)), 'bq_p': jnp.zeros((NH, HC), jnp.float32), 'wq_d': n(ks[2], (C, 1, 3, 3)), 'bq_d': jnp.zeros((C,), jnp.float32), 'wk_p': n(ks[3], (NH, HC, HC)), 'bk_p': jnp.zeros((NH, HC), jnp.float32), 'wk_d': n(ks[4], (C, 1, 3, 3)), 'bk_d': jnp.zeros((C,), jnp.float32), 'wv_p': n(ks[5], (NH, HC, HC)), 'bv_p': jnp.zeros((NH, HC), jnp.float32), 'wv_d': n(ks[6], (C, 1, 3, 3)), 'bv_d': jnp.zeros((C,), jnp.float32), 'alpha': jnp.ones((NH,), jnp.float32), 'w_f': n(ks[7], (C, C)), 'b_f': jnp.zeros((C,), jnp.float32)}
    _L1_conv_all = _L1_conv_setup()
    _L1_conv_in = {k: v for k, v in _L1_conv_all.items() if k in ('ln_g', 'ln_b', 'wq_p', 'bq_p', 'wq_d', 'bq_d', 'wk_p', 'bk_p', 'wk_d', 'bk_d', 'wv_p', 'bv_p', 'wv_d', 'bv_d', 'alpha', 'w_f', 'b_f')}
    del _L1_conv_all
    return {'x': x, 'L0_conv_qkv_w': _L0_conv_in['qkv_w'], 'L0_conv_qkv_b': _L0_conv_in['qkv_b'], 'L0_conv_proj_w': _L0_conv_in['proj_w'], 'L0_conv_proj_b': _L0_conv_in['proj_b'], 'L0_conv_rel_bias': _L0_conv_in['rel_bias'], 'L0_conv_norm1_g': _L0_conv_in['norm1_g'], 'L0_conv_norm1_b': _L0_conv_in['norm1_b'], 'L0_conv_norm2_g': _L0_conv_in['norm2_g'], 'L0_conv_norm2_b': _L0_conv_in['norm2_b'], 'L0_conv_fc1_w': _L0_conv_in['fc1_w'], 'L0_conv_fc1_b': _L0_conv_in['fc1_b'], 'L0_conv_fc2_w': _L0_conv_in['fc2_w'], 'L0_conv_fc2_b': _L0_conv_in['fc2_b'], 'L1_conv_ln_g': _L1_conv_in['ln_g'], 'L1_conv_ln_b': _L1_conv_in['ln_b'], 'L1_conv_wq_p': _L1_conv_in['wq_p'], 'L1_conv_bq_p': _L1_conv_in['bq_p'], 'L1_conv_wq_d': _L1_conv_in['wq_d'], 'L1_conv_bq_d': _L1_conv_in['bq_d'], 'L1_conv_wk_p': _L1_conv_in['wk_p'], 'L1_conv_bk_p': _L1_conv_in['bk_p'], 'L1_conv_wk_d': _L1_conv_in['wk_d'], 'L1_conv_bk_d': _L1_conv_in['bk_d'], 'L1_conv_wv_p': _L1_conv_in['wv_p'], 'L1_conv_bv_p': _L1_conv_in['bv_p'], 'L1_conv_wv_d': _L1_conv_in['wv_d'], 'L1_conv_bv_d': _L1_conv_in['bv_d'], 'L1_conv_alpha': _L1_conv_in['alpha'], 'L1_conv_w_f': _L1_conv_in['w_f'], 'L1_conv_b_f': _L1_conv_in['b_f']}

def reference(x, L0_conv_qkv_w, L0_conv_qkv_b, L0_conv_proj_w, L0_conv_proj_b, L0_conv_rel_bias, L0_conv_norm1_g, L0_conv_norm1_b, L0_conv_norm2_g, L0_conv_norm2_b, L0_conv_fc1_w, L0_conv_fc1_b, L0_conv_fc2_w, L0_conv_fc2_b, L1_conv_ln_g, L1_conv_ln_b, L1_conv_wq_p, L1_conv_bq_p, L1_conv_wq_d, L1_conv_bq_d, L1_conv_wk_p, L1_conv_bk_p, L1_conv_wk_d, L1_conv_bk_d, L1_conv_wv_p, L1_conv_bv_p, L1_conv_wv_d, L1_conv_bv_d, L1_conv_alpha, L1_conv_w_f, L1_conv_b_f):
    import jax
    import jax.numpy as jnp

    def _L0_conv_ref(x, qkv_w, qkv_b, proj_w, proj_b, rel_bias, norm1_g, norm1_b, norm2_g, norm2_b, fc1_w, fc1_b, fc2_w, fc2_b):
        import jax, jax.numpy as jnp
        import numpy as np
        DIM = 96
        HEADS = 12
        WS = 8
        SS = 4
        N = WS * WS
        HEAD_DIM = DIM // HEADS
        SCALE = HEAD_DIM ** (-0.5)
        MLP_HID = int(DIM * 4.0)

        def _relative_position_index():
            ch, cw = np.meshgrid(np.arange(WS), np.arange(WS), indexing='ij')
            coords = np.stack([ch, cw]).reshape(2, -1)
            rel = coords[:, :, None] - coords[:, None, :]
            rel = rel.transpose(1, 2, 0).astype(np.int64)
            rel[:, :, 0] += WS - 1
            rel[:, :, 1] += WS - 1
            rel[:, :, 0] *= 2 * WS - 1
            return jnp.asarray(rel.sum(-1))
        REL_IDX = _relative_position_index()

        def _shift_mask(H, W):
            img = np.zeros((H, W), dtype=np.float32)
            slices = (slice(0, -WS), slice(-WS, -SS), slice(-SS, None))
            cnt = 0
            for hs in slices:
                for ws_ in slices:
                    img[hs, ws_] = cnt
                    cnt += 1
            mw = img.reshape(H // WS, WS, W // WS, WS).transpose(0, 2, 1, 3).reshape(-1, N)
            diff = mw[:, None, :] - mw[:, :, None]
            return jnp.asarray(np.where(diff != 0, -10.0, 0.0).astype(np.float32))

        def _layernorm(x, g, b, eps=1e-05):
            mu = x.mean(-1, keepdims=True)
            var = ((x - mu) ** 2).mean(-1, keepdims=True)
            return (x - mu) * jax.lax.rsqrt(var + eps) * g + b
        B, C, H, W = x.shape
        x = x.transpose(0, 2, 3, 1)
        shortcut = x
        xn = _layernorm(x, norm1_g, norm1_b)
        xs = jnp.roll(xn, shift=(-SS, -SS), axis=(1, 2))
        nWh, nWw = (H // WS, W // WS)
        nW = nWh * nWw
        xw = xs.reshape(B, nWh, WS, nWw, WS, C).transpose(0, 1, 3, 2, 4, 5).reshape(B * nW, N, C)
        qkv = (xw @ qkv_w + qkv_b).reshape(B * nW, N, 3, HEADS, HEAD_DIM).transpose(2, 0, 3, 1, 4)
        q, k, v = (qkv[0] * SCALE, qkv[1], qkv[2])
        attn = jnp.einsum('bhnd,bhmd->bhnm', q, k)
        bias = rel_bias[REL_IDX.reshape(-1)].reshape(N, N, HEADS).transpose(2, 0, 1)
        attn = attn + bias[None]
        mask = _shift_mask(H, W)
        attn = attn.reshape(B, nW, HEADS, N, N) + mask[None, :, None]
        attn = attn.reshape(B * nW, HEADS, N, N)
        attn = jax.nn.softmax(attn, axis=-1)
        out = jnp.einsum('bhnm,bhmd->bhnd', attn, v).transpose(0, 2, 1, 3).reshape(B * nW, N, C)
        out = out @ proj_w + proj_b
        xs = out.reshape(B, nWh, nWw, WS, WS, C).transpose(0, 1, 3, 2, 4, 5).reshape(B, H, W, C)
        x = shortcut + jnp.roll(xs, shift=(SS, SS), axis=(1, 2))
        h = _layernorm(x, norm2_g, norm2_b)
        h = jax.nn.gelu(h @ fc1_w + fc1_b, approximate=False)
        x = x + (h @ fc2_w + fc2_b)
        return x.transpose(0, 3, 1, 2)

    def _L1_conv_ref(x, ln_g, ln_b, wq_p, bq_p, wq_d, bq_d, wk_p, bk_p, wk_d, bk_d, wv_p, bv_p, wv_d, bv_d, alpha, w_f, b_f):
        import jax, jax.numpy as jnp
        import numpy as np
        B, C, S, NH = (16, 96, 16, 8)
        HC = C // NH
        EPS = 1e-05

        def _dwconv(x, w, b):
            y = jax.lax.conv_general_dilated(x, w, window_strides=(1, 1), padding='SAME', feature_group_count=x.shape[1], dimension_numbers=('NCHW', 'OIHW', 'NCHW'))
            return y + b[None, :, None, None]

        def _proj(xn, wp, bp, wd, bd):
            b_, c_, s1, s2 = xn.shape
            xh = xn.reshape(b_, NH, HC, s1, s2)
            y = jnp.einsum('bhcij,hoc->bhoij', xh, wp) + bp[None, :, :, None, None]
            y = _dwconv(y.reshape(b_, c_, s1, s2), wd, bd).reshape(b_, NH, HC, s1, s2)
            return jnp.transpose(y, (0, 1, 4, 3, 2)).reshape(b_, NH, s2 * s1, HC)
        mu = jnp.mean(x, axis=(1, 2, 3), keepdims=True)
        var = jnp.mean((x - mu) ** 2, axis=(1, 2, 3), keepdims=True)
        xn = (x - mu) * jax.lax.rsqrt(var + EPS) * ln_g + ln_b
        Q = _proj(xn, wq_p, bq_p, wq_d, bq_d)
        K = _proj(xn, wk_p, bk_p, wk_d, bk_d)
        V = _proj(xn, wv_p, bv_p, wv_d, bv_d)
        logits = jnp.einsum('bhnc,bhnd->bhcd', K, Q) / alpha[None, :, None, None]
        attn = jax.nn.softmax(logits, axis=-1)
        out = jnp.einsum('bhnc,bhcd->bhnd', V, attn)
        b_, _, _, s = x.shape
        out = out.reshape(b_, NH, s, s, HC)
        out = jnp.transpose(out, (0, 1, 4, 3, 2)).reshape(b_, C, s, s)
        return jnp.einsum('bcij,oc->boij', out, w_f) + b_f[None, :, None, None] + xn

    def _gn(v, G=32, eps=1e-05):
        B_, C_, H_, W_ = v.shape
        g = v.reshape(B_, G, C_ // G, H_, W_)
        m = jnp.mean(g, axis=(2, 3, 4), keepdims=True)
        s = jnp.var(g, axis=(2, 3, 4), keepdims=True)
        return ((g - m) / jnp.sqrt(s + eps)).reshape(v.shape)

    def _ln_c(v, eps=1e-06):
        m = jnp.mean(v, axis=1, keepdims=True)
        s = jnp.var(v, axis=1, keepdims=True)
        return (v - m) / jnp.sqrt(s + eps)

    def _ln_t(v, eps=1e-05):
        m = jnp.mean(v, axis=-1, keepdims=True)
        s = jnp.var(v, axis=-1, keepdims=True)
        return (v - m) / jnp.sqrt(s + eps)

    def _to_tokens(v):
        B_, C_, H_, W_ = v.shape
        return v.reshape(B_, C_, H_ * W_).transpose(0, 2, 1)

    def _from_tokens(t, like):
        B_, C_, H_, W_ = like.shape
        return t.transpose(0, 2, 1).reshape(B_, C_, H_, W_)
    x = _L0_conv_ref(x, L0_conv_qkv_w, L0_conv_qkv_b, L0_conv_proj_w, L0_conv_proj_b, L0_conv_rel_bias, L0_conv_norm1_g, L0_conv_norm1_b, L0_conv_norm2_g, L0_conv_norm2_b, L0_conv_fc1_w, L0_conv_fc1_b, L0_conv_fc2_w, L0_conv_fc2_b)
    x = _L1_conv_ref(x, L1_conv_ln_g, L1_conv_ln_b, L1_conv_wq_p, L1_conv_bq_p, L1_conv_wq_d, L1_conv_bq_d, L1_conv_wk_p, L1_conv_bk_p, L1_conv_wk_d, L1_conv_bk_d, L1_conv_wv_p, L1_conv_bv_p, L1_conv_wv_d, L1_conv_bv_d, L1_conv_alpha, L1_conv_w_f, L1_conv_b_f)
    return x

_drawn_inputs = setup_inputs


def setup_inputs(seed=0):
    import zlib

    import numpy as np

    out = dict(_drawn_inputs(seed))
    spreads = {'L0_conv_qkv_b': (0.0, 0.1),
     'L0_conv_proj_b': (0.0, 0.1),
     'L0_conv_norm1_g': (1.0, 0.2),
     'L0_conv_norm1_b': (0.0, 0.1),
     'L0_conv_norm2_g': (1.0, 0.2),
     'L0_conv_norm2_b': (0.0, 0.1),
     'L0_conv_fc1_b': (0.0, 0.1),
     'L0_conv_fc2_b': (0.0, 0.1),
     'L1_conv_ln_g': (1.0, 0.2),
     'L1_conv_ln_b': (0.0, 0.1),
     'L1_conv_bq_p': (0.0, 0.8),
     'L1_conv_bq_d': (0.0, 0.319),
     'L1_conv_bk_p': (0.0, 0.8),
     'L1_conv_bk_d': (0.0, 0.358),
     'L1_conv_bv_p': (0.0, 0.8),
     'L1_conv_bv_d': (0.0, 0.296),
     'L1_conv_alpha': (1.0, 0.6),
     'L1_conv_b_f': (0.0, 0.1)}
    factors = {'L0_conv_rel_bias': 8.0,
     'L1_conv_wq_p': 8.0,
     'L1_conv_wq_d': 8.0,
     'L1_conv_wk_p': 8.0,
     'L1_conv_wk_d': 8.0,
     'L1_conv_wv_p': 7.445,
     'L1_conv_wv_d': 6.502}
    for name, (base, spread) in spreads.items():
        noise = np.random.default_rng([zlib.crc32(name.encode()), seed]).standard_normal(out[name].shape)
        drawn = base * np.exp(spread * noise) if base else spread * noise
        out[name] = jnp.asarray(drawn.astype(out[name].dtype))
    for name, factor in factors.items():
        out[name] = (out[name] * factor).astype(out[name].dtype)
    return out
```

```python
from contextlib import ExitStack

import numpy as np

import concourse.bass as bass
from concourse import mybir

ALU = mybir.AluOpType
ACT = mybir.ActivationFunctionType
AX_X = mybir.AxisListType.X
F32 = mybir.dt.float32

B, C, H, W = 32, 96, 16, 16
N = H * W
HEADS, HD = 12, 8
WS, SS = 8, 4
WN = WS * WS
GROUP = 4
NG = HEADS // GROUP
PAIRS = 2
HP = HEADS // 2
SC = HEADS * WN
VC = HD + 1
HID = 4 * C
HT = HID // 128
REL = 2 * WS - 1
NH2, HC = 8, 12
EPS = 1e-5
SCALE = HD ** -0.5
PADW = W + 2
TAPS = 9
CHUNK = 2 * N
BLOCKED = -1e30


def need(engine, semaphore, count):
    if isinstance(count, int) and count <= 0:
        return
    engine.wait_ge(semaphore, count)


def image_loop(engine, step):
    step(0, 0, 0)
    step(1, 0, 1)
    with engine.Fori(1, B // 2 - 1) as i:
        step(i * 2, i, 0)
        step(i * 2 + 1, i, 1)
    step(B - 2, B // 2 - 1, 0)
    step(B - 1, B // 2 - 1, 1)


def is_image(t, other):
    return isinstance(t, int) and t == other


def build(nc, a, debug=None):
    ctx = ExitStack()
    with ctx:
        def sb(name, shape, dt=F32):
            return ctx.enter_context(nc.sbuf_tensor(name, shape, dt))

        def sem(name):
            return ctx.enter_context(nc.semaphore(name))

        stream = sb("stream", [C, B * N])
        ident = sb("ident", [128, 128])
        center = sb("center", [C, C])
        average = sb("average", [C, C])
        w = {name: sb(name, shape) for name, shape in (
            ("fc1", [C, HID]), ("fc2", [128, HT, C]), ("fc1_b", [128, HT]), ("fc2_b", [C, 1]),
            ("norm2_g", [C, 1]), ("norm2_b", [C, 1]),
            ("ln_g", [C, N]), ("ln_b", [C, N]),
            ("point_q", [C, C]), ("point_k", [C, C]), ("point_v", [C, C]), ("final", [C, C]),
            ("point_b", [C, 3]), ("taps", [C, 3, TAPS]), ("taps_b", [C, 3]), ("alpha", [C, 1]), ("final_b", [C, 1]),
            ("block_mask", [C, C]))}
        weights_in = sem("weights_in")
        zeroed_points = sem("zeroed_points")
        with ExitStack() as p1:
            window_attention(nc, p1, a, sem, stream, ident, center, average, w, weights_in, zeroed_points)
        if debug == 1:
            dump(nc, sem, stream, a["out"])
            return
        mixed = sb("mixed", [C, B * N])
        stats = sb("stats", [C, B, 6])
        with ExitStack() as p2:
            mlp(nc, p2, sem, stream, mixed, stats, center, average, w)
        if debug == 2:
            dump(nc, sem, mixed, a["out"])
            return
        with ExitStack() as p3:
            channel_attention(nc, p3, sem, mixed, stats, ident, average, w, a["out"])


def dump(nc, sem, stream, out):
    done = sem("dumped")
    with nc.Block() as block:
        @block.sync
        def _(sp):
            for t in range(B):
                sp.dma_start(out[t].rearrange("c h w -> c (h w)"), stream[:, t * N:(t + 1) * N]).then_inc(done, 16)
            sp.wait_ge(done, 16 * B)


def grid(ap, width=W):
    return ap.rearrange("p (r c) -> p r c", c=width)


def windows(ap):
    return ap.rearrange("p (a w r c) -> p a w r c", a=2, w=2, r=WS)


def weight_loads(a, w):
    def column(name, k=0, n=C):
        return a[name][k * n:(k + 1) * n].rearrange("(c a) -> c a", a=1)

    loads = [
        (w["fc1"][:, :], a["L0_conv_fc1_w"]),
        (w["fc2"][:, :, :], a["L0_conv_fc2_w"].rearrange("(k p) c -> p k c", p=128)),
        (w["fc2_b"][:, :], column("L0_conv_fc2_b")),
        (w["norm2_g"][:, :], column("L0_conv_norm2_g")),
        (w["norm2_b"][:, :], column("L0_conv_norm2_b")),
        (w["ln_g"][:, :], a["L1_conv_ln_g"].rearrange("c h w -> c (h w)")),
        (w["ln_b"][:, :], a["L1_conv_ln_b"].rearrange("c h w -> c (h w)")),
        (w["final"][:, :], a["L1_conv_w_f"]),
        (w["final_b"][:, :], column("L1_conv_b_f")),
        (w["block_mask"][:, :], a["c_block_mask"]),
    ]
    loads += [(w["fc1_b"][:, k:k + 1], column("L0_conv_fc1_b", k, 128)) for k in range(HT)]
    for k, n in enumerate("qkv"):
        loads += [
            (w["point_b"][:, k:k + 1], a[f"L1_conv_b{n}_p"].rearrange("h (c a) -> (h c) a", a=1)),
            (w["taps"][:, k, :], a[f"L1_conv_w{n}_d"].rearrange("c a i j -> c (a i j)")),
            (w["taps_b"][:, k:k + 1], column(f"L1_conv_b{n}_d")),
        ]
        loads += [(w[f"point_{n}"][h * HC:(h + 1) * HC, h * HC:(h + 1) * HC], a[f"L1_conv_w{n}_p"][h])
                  for h in range(NH2)]
    loads += [(w["alpha"][h * HC:(h + 1) * HC, :],
               a["L1_conv_alpha"][h:h + 1].rearrange("(b a) -> b a", a=1).to_broadcast((HC, 1))) for h in range(NH2)]
    return loads


def window_attention(nc, ctx, a, sem, stream, ident, center, average, w_late, weights_in, zeroed_points):
    def sb(name, shape, dt=F32):
        return ctx.enter_context(nc.sbuf_tensor(name, shape, dt))

    def bank(name, count=1):
        return ctx.enter_context(nc.psum_tensor(name, [128, count, 512], F32))

    head_mask = sb("head_mask", [C, GROUP])
    shift_mask = sb("shift_mask", [128, PAIRS, WN])
    rel_rows = sb("rel_rows", [128, WN, HEADS])
    bias = sb("bias", [128, PAIRS, SC])
    w_in = sb("w_in", [C, 3 * C])
    w_qkv = sb("w_qkv", [C, 3 * C])
    w_proj = sb("w_proj", [C, C])
    cols = sb("cols", [C, 7])
    b_q = sb("b_q", [C, 1])
    b_k = sb("b_k", [C, 1])
    b_v = sb("b_v", [C, 1])
    b_kj = sb("b_kj", [C, GROUP])
    b_proj = sb("b_proj", [C, 1])
    x_in = sb("x_in", [C, 2, N])
    squares = sb("squares", [C, N])
    log_var = sb("log_var", [C, N])
    eps = sb("eps", [C, 1])
    rstd = sb("rstd", [C, N])
    normed = sb("normed", [C, 2 * PAIRS, 2, WN])
    q_sb = sb("q_sb", [C, N])
    k_blocks = sb("k_blocks", [C, GROUP, N])
    v_blocks = sb("v_blocks", [128, 2, 2 * PAIRS, HP, 2, VC])
    scores = sb("scores", [128, PAIRS, SC])
    peak = sb("peak", [128, PAIRS, HEADS])
    probs_t = sb("probs_t", [128, SC])
    recip = sb("recip", [128, HEADS])
    heads_out = sb("heads_out", [128, C])
    out_t = sb("out_t", [C, N])

    ps_scores = bank("ps_scores", NG)
    ps_probs = bank("ps_probs", 2)
    ps_out = bank("ps_out")
    ps_a = bank("ps_a")
    ps_b = bank("ps_b")
    centred = ps_a[0:C, 0, 0:N]
    ps_q = ps_a[0:C, 0, 0:N]
    ps_k = ps_a[0:C, 0, N:2 * N]
    ps_var = ps_b[0:C, 0, 0:N]
    ps_v = ps_b[:, 0, 0:2 * PAIRS * C].rearrange("p (w c) -> p w c", c=C)
    ps_proj = ps_b[0:C, 0, 0:N]
    ps_pv = ps_out[:, 0, 0:HP * 4 * VC].rearrange("p (q w e c) -> p q w e c", q=HP, w=2, e=2)
    ps_ot = ps_out[0:C, 0, 256:384]

    consts_in = sem("consts_in")
    rel_in = sem("rel_in")
    rel_dup = sem("rel_dup")
    set_up = sem("set_up")
    pe_set = sem("pe_set")
    zeroed = sem("zeroed")
    x_landed = [sem("x_landed0"), sem("x_landed1")]
    s = {n: sem(n) for n in (
        "rolled", "centred_ready", "squares_ready", "var_ready", "log_ready", "rstd_ready", "normed_ready",
        "qk_ready", "q_copied", "k_copied_act", "k_copied_dve", "v_ready", "v_copied",
        "scores_ready", "biased", "peak_ready", "shifted", "probs_ready", "turned", "turned_copied",
        "pv_ready", "recip_ready", "heads_ready", "ot_ready", "ot_copied", "proj_ready", "residual_done")}

    x = a["x"]
    block = ctx.enter_context(nc.Block())

    @block.sync
    def _(sp):
        for dst, src in (
            (ident[:, :], a["c_ident"]), (center[:, :], a["c_center"]), (average[:, :], a["c_average"]),
            (head_mask[:, :], a["c_head_mask"]), (shift_mask[:, :, :], a["c_shift_mask"]),
            (w_in[:, :], a["L0_conv_qkv_w"]), (w_proj[:, :], a["L0_conv_proj_w"]),
            (cols[:, 0:1], a["L0_conv_norm1_g"].rearrange("(c a) -> c a", a=1)),
            (cols[:, 1:2], a["L0_conv_norm1_b"].rearrange("(c a) -> c a", a=1)),
            *((cols[:, 2 + k:3 + k], a["L0_conv_qkv_b"][k * C:(k + 1) * C].rearrange("(c a) -> c a", a=1))
              for k in range(3)),
            (cols[:, 5:6], a["L0_conv_proj_b"].rearrange("(c a) -> c a", a=1)),
        ):
            sp.dma_start(dst, src).then_inc(consts_in, 16)

        late = weight_loads(a, w_late)

        def step(t, half, par):
            need(sp, s["rolled"], (t - 1) * 3)
            xt = x[bass.ds(t, 1)] if not isinstance(t, int) else x[t:t + 1]
            xt = xt.rearrange("a c h w -> c (a h w)")
            sp.dma_start(x_in[:, par, 0:N - SS * W], xt[:, SS * W:N]).then_inc(x_landed[par], 16)
            sp.dma_start(x_in[:, par, N - SS * W:N], xt[:, 0:SS * W]).then_inc(x_landed[par], 16)

        image_loop(sp, step)
        sp.wait_ge(zeroed_points, 3)
        for dst, src in late:
            sp.dma_start(dst, src).then_inc(weights_in, 16)
        sp.wait_ge(weights_in, 16 * len(late))

    @block.gpsimd
    def _(pool):
        for n in "qkv":
            nc.gpsimd.memset(w_late[f"point_{n}"][:, :], 0.0).then_inc(zeroed_points, 1)
        nc.gpsimd.memset(v_blocks[:, :, :, :, :, :], 0.0).then_inc(zeroed, 1)
        nc.gpsimd.memset(eps[:, :], EPS).then_inc(zeroed, 1)
        pool.wait_ge(zeroed, 2)
        for e in range(2):
            for par in range(2):
                nc.gpsimd.memset(v_blocks[64 * e:64 * e + 64, par, :, :, e, HD:VC], 1.0).then_inc(zeroed, 1)

        def subtract_peak(t, p):
            u = t * 2 + p
            pool.wait_ge(s["peak_ready"], u + 1)
            sc = scores[:, p, :].rearrange("p (h m) -> p h m", m=WN)
            nc.gpsimd.tensor_tensor(sc, sc, peak[:, p, :].unsqueeze(2).to_broadcast((128, HEADS, WN)),
                                    ALU.subtract).then_inc(s["shifted"], 1)

        subtract_peak(0, 0)

        def step(t, half, par):
            subtract_peak(t, 1)
            if not is_image(t, B - 1):
                subtract_peak(t + 1, 0)

        image_loop(pool, step)

    @block.scalar
    def _(act):
        table = a["L0_conv_rel_bias"].rearrange("(r c) h -> r (c h)", c=REL)
        for y in range(WS):
            for x_at in range(WS):
                act.dma_start(rel_rows[y * WS + x_at:y * WS + x_at + 1, :, :].rearrange("p (r c) h -> p r (c h)", r=WS),
                              table[y:y + WS, x_at * HEADS:(x_at + WS) * HEADS].unsqueeze(0)).then_inc(rel_in, 16)
        act.wait_ge(rel_in, 16 * WN)
        act.dma_start(rel_rows[WN:128, :, :], rel_rows[0:WN, :, :]).then_inc(rel_dup, 16)

        def square(t):
            act.wait_ge(s["centred_ready"], t + 1)
            need(act, s["var_ready"], t)
            nc.scalar.activation(squares[:, :], centred, ACT.Square).then_inc(s["squares_ready"], 1)

        def inverse_deviation(t):
            act.wait_ge(s["var_ready"], t + 1)
            need(act, s["rstd_ready"], t)
            nc.scalar.activation(log_var[:, :], ps_var, ACT.Ln, bias=eps[:, 0:1]).then_inc(s["log_ready"], 1)
            act.wait_ge(s["log_ready"], t + 1)
            need(act, s["normed_ready"], t)
            nc.scalar.activation(rstd[:, :], log_var[:, :], ACT.Exp, scale=-0.5).then_inc(s["rstd_ready"], 1)

        def copy_q_k(t):
            act.wait_ge(s["qk_ready"], t + 1)
            need(act, s["scores_ready"], t * 2)
            nc.scalar.activation(q_sb[:, :], ps_q, ACT.Identity, bias=b_q[:, 0:1], scale=SCALE).then_inc(s["q_copied"], 1)
            for j in range(2):
                nc.scalar.activation(k_blocks[:, j, :], ps_k, ACT.Identity, bias=b_kj[:, j:j + 1],
                                     scale=head_mask[:, j:j + 1]).then_inc(s["k_copied_act"], 1)

        def exponent(t, p):
            act.wait_ge(s["shifted"], t * 2 + p + 1)
            nc.scalar.activation(scores[:, p, :], scores[:, p, :], ACT.Exp).then_inc(s["probs_ready"], 1)

        def copy_turned(t, p):
            u = t * 2 + p
            act.wait_ge(s["turned"], u + 1)
            need(act, s["pv_ready"], u)
            nc.scalar.copy(probs_t[:, :].rearrange("p (k c) -> p k c", k=2), ps_probs[:, :, 0:SC // 2]).then_inc(s["turned_copied"], 1)

        def copy_ot(t, p):
            act.wait_ge(s["ot_ready"], t * 2 + p + 1)
            need(act, s["proj_ready"], t)
            nc.scalar.copy(out_t[:, p * 2 * WN:(p + 1) * 2 * WN], ps_ot).then_inc(s["ot_copied"], 1)

        nc.scalar.preload_act_table_set("natural_log_exp_and_others")
        act.wait_ge(zeroed, 6)
        act.wait_ge(set_up, 7)
        square(0)
        inverse_deviation(0)
        copy_q_k(0)
        exponent(0, 0)

        def step(t, half, par):
            last = is_image(t, B - 1)
            if not last:
                square(t + 1)
            if not is_image(t, 0):
                copy_ot(t - 1, 1)
            copy_turned(t, 0)
            if not last:
                inverse_deviation(t + 1)
            exponent(t, 1)
            if not last:
                copy_q_k(t + 1)
            copy_ot(t, 0)
            copy_turned(t, 1)
            if not last:
                exponent(t + 1, 0)

        image_loop(act, step)
        copy_ot(B - 1, 1)

    @block.vector
    def _(dve):
        def fold(k):
            dve.wait_ge(set_up, k)

        dve.wait_ge(consts_in, 16 * 13)
        nc.vector.tensor_scalar(w_qkv[:, :], w_in[:, :], cols[:, 0:1], None, ALU.mult).then_inc(set_up, 1)
        dve.wait_ge(pe_set, 3)
        nc.vector.tensor_tensor(b_q[:, :], ps_a[0:C, 0, 0:1], cols[:, 2:3], ALU.add).then_inc(set_up, 1)
        nc.vector.tensor_tensor(b_k[:, :], ps_a[0:C, 0, 1:2], cols[:, 3:4], ALU.add).then_inc(set_up, 1)
        nc.vector.tensor_tensor(b_v[:, :], ps_a[0:C, 0, 2:3], cols[:, 4:5], ALU.add).then_inc(set_up, 1)
        fold(3)
        nc.vector.tensor_scalar(b_q[:, :], b_q[:, :], SCALE, None, ALU.mult).then_inc(set_up, 1)
        nc.vector.tensor_scalar(b_kj[:, :], head_mask[:, :], b_k[:, 0:1], None, ALU.mult).then_inc(set_up, 1)
        dve.wait_ge(pe_set, 4)
        nc.vector.tensor_tensor(b_proj[:, :], ps_b[0:C, 0, 0:1], cols[:, 5:6], ALU.add).then_inc(set_up, 1)
        dve.wait_ge(rel_dup, 16)
        for p in range(PAIRS):
            nc.vector.tensor_tensor(bias[:, p, :].rearrange("p (h m) -> p h m", m=WN),
                                    rel_rows[:, ::-1, :].rearrange("p m h -> p h m"),
                                    shift_mask[:, p, :].unsqueeze(1).to_broadcast((128, HEADS, WN)),
                                    ALU.add).then_inc(set_up, 1)
        dve.wait_ge(zeroed, 6)

        def roll(t, half, par):
            dve.wait_ge(x_landed[par], (half + 1) * 32)
            src = grid(x_in[:, par, :])
            dst = windows(stream[:, bass.ds(t * N, N)])
            for w, c0, n, at in ((0, 0, WS, SS), (1, 0, SS, WS + SS), (1, SS, SS, 0)):
                nc.vector.tensor_copy(dst[:, :, w, :, c0:c0 + n],
                                      src[:, :, at:at + n].rearrange("p (a r) c -> p a r c", a=2)).then_inc(s["rolled"], 1)

        def normalise(t):
            dve.wait_ge(s["rstd_ready"], t + 1)
            need(dve, s["v_ready"], t)
            def twice(ap):
                return ap.rearrange("p (w m) -> p w m", m=WN).unsqueeze(2).to_broadcast((C, 2 * PAIRS, 2, WN))
            nc.vector.tensor_tensor(normed[:, :, :, :], twice(centred), twice(rstd[:, :]),
                                    ALU.mult).then_inc(s["normed_ready"], 1)

        def copy_k(t):
            dve.wait_ge(s["qk_ready"], t + 1)
            dve.wait_ge(s["k_copied_act"], (t + 1) * 2)
            need(dve, s["scores_ready"], t * 2)
            for j in range(2, GROUP):
                nc.vector.tensor_scalar(k_blocks[:, j, :], ps_k, b_k[:, 0:1], head_mask[:, j:j + 1],
                                        ALU.add, ALU.mult).then_inc(s["k_copied_dve"], 1)

        def copy_v(t, par):
            dve.wait_ge(s["v_ready"], t + 1)
            need(dve, s["pv_ready"], (t - 1) * 2)
            for e in range(2):
                src = ps_v[64 * e:64 * e + 64].rearrange("p w (q e d) -> p w q e d", q=HP, e=2)
                nc.vector.tensor_copy(v_blocks[64 * e:64 * e + 64, par, :, :, e, 0:HD],
                                      src[:, :, :, e, :]).then_inc(s["v_copied"], 1)

        def add_bias(t, p):
            u = t * 2 + p
            dve.wait_ge(s["scores_ready"], u + 1)
            need(dve, s["turned"], u - 1)
            nc.vector.tensor_tensor(scores[:, p, :].rearrange("p (g c) -> p g c", g=NG),
                                    ps_scores[:, :, 0:GROUP * WN],
                                    bias[:, p, :].rearrange("p (g c) -> p g c", g=NG), ALU.add).then_inc(s["biased"], 1)
            dve.wait_ge(s["biased"], u + 1)
            need(dve, s["shifted"], u - 1)
            nc.vector.tensor_reduce(peak[:, p, :], scores[:, p, :].rearrange("p (h m) -> p h m", m=WN),
                                    AX_X, ALU.max).then_inc(s["peak_ready"], 1)

        def weigh_heads(t, p):
            u = t * 2 + p
            dve.wait_ge(s["pv_ready"], u + 1)
            need(dve, s["heads_ready"], u * 2)
            for w in range(2):
                rows = slice(64 * w, 64 * w + 64)
                nc.vector.reciprocal(recip[rows, :].rearrange("p (q e) -> p q e", e=2),
                                     ps_pv[rows, :, w, :, HD]).then_inc(s["recip_ready"], 1)
            dve.wait_ge(s["recip_ready"], (u + 1) * 2)
            need(dve, s["ot_ready"], u)
            for w in range(2):
                rows = slice(64 * w, 64 * w + 64)
                r = recip[rows, :].rearrange("p (q e) -> p q e", e=2).unsqueeze(3).to_broadcast((64, HP, 2, HD))
                nc.vector.tensor_tensor(heads_out[rows, :].rearrange("p (q e d) -> p q e d", q=HP, e=2),
                                        ps_pv[rows, :, w, :, 0:HD], r, ALU.mult).then_inc(s["heads_ready"], 1)

        def add_residual(t):
            dve.wait_ge(s["proj_ready"], t + 1)
            dst = stream[:, bass.ds(t * N, N)]
            nc.vector.scalar_tensor_tensor(out=dst, in0=ps_proj, scalar=b_proj[:, 0:1], in1=dst,
                                           op0=ALU.add, op1=ALU.add).then_inc(s["residual_done"], 1)

        roll(0, 0, 0)
        roll(1, 0, 1)
        normalise(0)
        copy_k(0)
        copy_v(0, 0)
        add_bias(0, 0)

        def step(t, half, par):
            last = is_image(t, B - 1)
            if not last and not is_image(t, B - 2):
                roll(t + 2, half + 1, par)
            add_bias(t, 1)
            if not last:
                normalise(t + 1)
            weigh_heads(t, 0)
            if not is_image(t, 0):
                add_residual(t - 1)
            if not last:
                copy_k(t + 1)
                copy_v(t + 1, 1 - par)
                add_bias(t + 1, 0)
            weigh_heads(t, 1)

        image_loop(dve, step)
        add_residual(B - 1)

    @block.tensor
    def _(pe):
        pe.wait_ge(consts_in, 16 * 13)
        for k in range(3):
            nc.tensor.matmul(ps_a[0:C, 0, k:k + 1], w_in[:, k * C:(k + 1) * C], cols[:, 1:2],
                             start=True, stop=True, skip_group_check=True).then_inc(pe_set, 1)
        pe.wait_ge(set_up, 4)
        nc.tensor.matmul(ps_b[0:C, 0, 0:1], w_proj[:, :], b_v[:, 0:1], start=True, stop=True).then_inc(pe_set, 1)
        pe.wait_ge(set_up, 7)

        def centre(t):
            pe.wait_ge(s["rolled"], (t + 1) * 3)
            need(pe, s["q_copied"], t)
            need(pe, s["k_copied_dve"], t * 2)
            nc.tensor.matmul(centred, center[:, :], stream[:, bass.ds(t * N, N)],
                             start=True, stop=True).then_inc(s["centred_ready"], 1)

        def spread(t):
            pe.wait_ge(s["squares_ready"], t + 1)
            need(pe, s["v_copied"], t * 2)
            nc.tensor.matmul(ps_var, average[:, :], squares[:, :], start=True, stop=True).then_inc(s["var_ready"], 1)

        def make_q_k(t):
            pe.wait_ge(s["normed_ready"], t + 1)
            nc.tensor.matmul(ps_q, w_qkv[:, 0:C], normed[:, :, 0, :], start=True, stop=True)
            nc.tensor.matmul(ps_k, w_qkv[:, C:2 * C], normed[:, :, 0, :], start=True, stop=True,
                             skip_group_check=True).then_inc(s["qk_ready"], 1)

        def make_v(t):
            pe.wait_ge(s["normed_ready"], t + 1)
            pe.wait_ge(s["log_ready"], t + 1)
            need(pe, s["residual_done"], t - 1)
            for w in range(2 * PAIRS):
                twice = normed[:, w, :, :].rearrange("p e m -> p (e m)")
                mm = nc.tensor.matmul(ps_v[:, w, :], twice, w_qkv[:, 2 * C:3 * C], start=True, stop=True,
                                      skip_group_check=True)
            mm.then_inc(s["v_ready"], 1)

        def score(t, p):
            u = t * 2 + p
            pe.wait_ge(s["q_copied"], t + 1)
            pe.wait_ge(s["k_copied_act"], (t + 1) * 2)
            pe.wait_ge(s["k_copied_dve"], (t + 1) * 2)
            need(pe, s["biased"], u)
            for g in range(NG):
                ch = slice(32 * g, 32 * g + 32)
                for w in range(2):
                    tokens = slice((2 * p + w) * WN, (2 * p + w + 1) * WN)
                    q, k = q_sb[ch, tokens], k_blocks[ch, :, tokens]
                    mm = nc.tensor.matmul(ps_scores[64 * w:64 * w + 64, g, 0:GROUP * WN], q, k, start=True, stop=True)
            mm.then_inc(s["scores_ready"], 1)

        def turn(t, p):
            u = t * 2 + p
            pe.wait_ge(s["probs_ready"], u + 1)
            need(pe, s["turned_copied"], u)
            for q in range(HP):
                mm = nc.tensor.transpose(ps_probs[:, q // 3, (q % 3) * 128:(q % 3 + 1) * 128],
                                         scores[:, p, q * 128:(q + 1) * 128], ident[:, :])
            mm.then_inc(s["turned"], 1)

        def weigh(t, p, par):
            u = t * 2 + p
            pe.wait_ge(s["turned_copied"], u + 1)
            pe.wait_ge(s["v_copied"], (t + 1) * 2)
            need(pe, s["ot_copied"], u)
            for q in range(HP):
                mm = nc.tensor.matmul(ps_pv[:, q], probs_t[:, q * 128:(q + 1) * 128],
                                      v_blocks[:, par, 2 * p:2 * p + 2, q, :, :], start=True, stop=True,
                                      skip_group_check=True)
            mm.then_inc(s["pv_ready"], 1)

        def turn_heads(t, p):
            u = t * 2 + p
            pe.wait_ge(s["heads_ready"], (u + 1) * 2)
            nc.tensor.transpose(ps_ot, heads_out[:, :], ident[:, :]).then_inc(s["ot_ready"], 1)

        def project(t, spreads):
            pe.wait_ge(s["ot_copied"], (t + 1) * 2)
            pe.wait_ge(s["log_ready"], spreads)
            nc.tensor.matmul(ps_proj, w_proj[:, :], out_t[:, :], start=True, stop=True).then_inc(s["proj_ready"], 1)

        centre(0)
        spread(0)
        make_q_k(0)
        make_v(0)
        score(0, 0)

        def step(t, half, par):
            last = is_image(t, B - 1)
            score(t, 1)
            if not last:
                centre(t + 1)
            if not is_image(t, 0):
                turn_heads(t - 1, 1)
            turn(t, 0)
            if not last:
                spread(t + 1)
            weigh(t, 0, par)
            if not is_image(t, 0):
                project(t - 1, B if last else t + 2)
            if not last:
                make_q_k(t + 1)
            turn_heads(t, 0)
            turn(t, 1)
            if not last:
                make_v(t + 1)
                score(t + 1, 0)
            weigh(t, 1, par)

        image_loop(pe, step)
        turn_heads(B - 1, 1)
        project(B - 1, B)


def chunk_loop(engine, step):
    n = B * N // CHUNK
    step(0, 0, 0)
    step(1, 0, 1)
    with engine.Fori(1, n // 2 - 1) as i:
        step(i * 2, i, 0)
        step(i * 2 + 1, i, 1)
    step(n - 2, n // 2 - 1, 0)
    step(n - 1, n // 2 - 1, 1)


def mlp(nc, ctx, sem, stream, mixed, stats, center, average, w):
    CHUNKS = B * N // CHUNK

    def sb(name, shape, dt=F32):
        return ctx.enter_context(nc.sbuf_tensor(name, shape, dt))

    with ExitStack() as norm:
        ps_centred = norm.enter_context(nc.psum_tensor("ps_centred", [128, 2, CHUNK], F32))
        ps_var = norm.enter_context(nc.psum_tensor("ps_var2", [128, 2, CHUNK], F32))
        squares, log_var, rstd = (norm.enter_context(nc.sbuf_tensor(n, [C, 2, CHUNK], F32))
                                  for n in ("squares2", "log_var2", "rstd2"))
        eps = norm.enter_context(nc.sbuf_tensor("eps2", [C, 1], F32))
        eps_set = sem("eps_set")
        s = {n: sem(n + "_2") for n in ("centred_ready", "squares_ready", "var_ready", "log_ready",
                                        "rstd_ready", "normed_ready")}
        with nc.Block() as block:
            @block.gpsimd
            def _(pool):
                nc.gpsimd.memset(eps[:, :], EPS).then_inc(eps_set, 1)

            @block.tensor
            def _(pe):
                def centre(k, par):
                    need(pe, s["normed_ready"], k - 1)
                    nc.tensor.matmul(ps_centred[0:C, par, :], center[:, :], stream[:, bass.ds(k * CHUNK, CHUNK)],
                                     start=True, stop=True).then_inc(s["centred_ready"], 1)

                def spread(k, par):
                    pe.wait_ge(s["squares_ready"], k + 1)
                    need(pe, s["log_ready"], k - 1)
                    nc.tensor.matmul(ps_var[0:C, par, :], average[:, :], squares[:, par, :],
                                     start=True, stop=True).then_inc(s["var_ready"], 1)

                def step(k, half, par):
                    if not is_image(k, CHUNKS - 1):
                        centre(k + 1, 1 - par)
                    spread(k, par)

                centre(0, 0)
                chunk_loop(pe, step)

            @block.scalar
            def _(act):
                act.wait_ge(eps_set, 1)

                def square(k, par):
                    act.wait_ge(s["centred_ready"], k + 1)
                    need(act, s["var_ready"], k - 1)
                    nc.scalar.activation(squares[:, par, :], ps_centred[0:C, par, :],
                                         ACT.Square).then_inc(s["squares_ready"], 1)

                def step(k, half, par):
                    if not is_image(k, CHUNKS - 1):
                        square(k + 1, 1 - par)
                    act.wait_ge(s["var_ready"], k + 1)
                    need(act, s["rstd_ready"], k - 1)
                    nc.scalar.activation(log_var[:, par, :], ps_var[0:C, par, :], ACT.Ln,
                                         bias=eps[:, 0:1]).then_inc(s["log_ready"], 1)
                    act.wait_ge(s["log_ready"], k + 1)
                    need(act, s["normed_ready"], k - 1)
                    nc.scalar.activation(rstd[:, par, :], log_var[:, par, :], ACT.Exp,
                                         scale=-0.5).then_inc(s["rstd_ready"], 1)

                nc.scalar.preload_act_table_set("natural_log_exp_and_others")
                square(0, 0)
                chunk_loop(act, step)

            @block.vector
            def _(dve):
                def step(k, half, par):
                    dve.wait_ge(s["rstd_ready"], k + 1)
                    nc.vector.tensor_tensor(mixed[:, bass.ds(k * CHUNK, CHUNK)], ps_centred[0:C, par, :],
                                            rstd[:, par, :], ALU.mult).then_inc(s["normed_ready"], 1)

                chunk_loop(dve, step)

    fc1 = sb("fc1_scaled", [C, HID])
    fc1_b = sb("fc1_b_folded", [128, HT])
    summed = sb("summed", [C, 2, CHUNK])
    hidden = sb("hidden", [128, 2, HT, CHUNK])
    ps_hidden = ctx.enter_context(nc.psum_tensor("ps_hidden", [128, 2 * HT, CHUNK], F32))
    ps_y = ctx.enter_context(nc.psum_tensor("ps_y", [128, 2, CHUNK], F32))
    set_up = sem("set_up_mlp")
    pe_set = sem("pe_set_mlp")
    s = {n: sem(n) for n in ("hidden_ready", "gelu_ready", "y_ready", "sum_ready", "mixed_ready", "stats_ready")}
    QUARTERS = 4
    block = ctx.enter_context(nc.Block())

    @block.tensor
    def _(pe):
        for k in range(HT):
            nc.tensor.matmul(ps_y[:, 0, k:k + 1], w["fc1"][:, k * 128:(k + 1) * 128], w["norm2_b"][:, :],
                             start=True, stop=True, skip_group_check=True).then_inc(pe_set, 1)
        pe.wait_ge(set_up, 2)

        def up(k, par):
            need(pe, s["gelu_ready"], (k - 1) * HT)
            for h in range(HT):
                nc.tensor.matmul(ps_hidden[:, par * HT + h, :], fc1[:, h * 128:(h + 1) * 128],
                                 mixed[:, bass.ds(k * CHUNK, CHUNK)], start=True, stop=True).then_inc(s["hidden_ready"], 1)

        def down(k, par):
            need(pe, s["sum_ready"], k - 1)
            for h in range(HT):
                pe.wait_ge(s["gelu_ready"], k * HT + h + 1)
                mm = nc.tensor.matmul(ps_y[0:C, par, :], w["fc2"][:, h, :], hidden[:, par, h, :],
                                      start=(h == 0), stop=(h == HT - 1))
            mm.then_inc(s["y_ready"], 1)

        def step(k, half, par):
            if not is_image(k, CHUNKS - 1):
                up(k + 1, 1 - par)
            down(k, par)

        up(0, 0)
        chunk_loop(pe, step)

    @block.scalar
    def _(act):
        act.wait_ge(set_up, 2)

        def step(k, half, par):
            need(act, s["y_ready"], k - 1)
            for h in range(HT):
                act.wait_ge(s["hidden_ready"], k * HT + h + 1)
                nc.scalar.activation(hidden[:, par, h, :], ps_hidden[:, par * HT + h, :], ACT.Gelu,
                                     bias=fc1_b[:, h:h + 1]).then_inc(s["gelu_ready"], 1)

        chunk_loop(act, step)

    @block.vector
    def _(dve):
        nc.vector.tensor_scalar(fc1[:, :], w["fc1"][:, :], w["norm2_g"][:, 0:1], None, ALU.mult).then_inc(set_up, 1)
        dve.wait_ge(pe_set, HT)
        nc.vector.tensor_tensor(fc1_b[:, :], ps_y[:, 0, 0:HT], w["fc1_b"][:, :], ALU.add).then_inc(set_up, 1)

        def step(k, half, par):
            dve.wait_ge(s["y_ready"], k + 1)
            need(dve, s["mixed_ready"], (k - 1) * 2 * QUARTERS)
            nc.vector.scalar_tensor_tensor(out=summed[:, par, :], in0=ps_y[0:C, par, :], scalar=w["fc2_b"][:, 0:1],
                                           in1=stream[:, bass.ds(k * CHUNK, CHUNK)],
                                           op0=ALU.add, op1=ALU.add).then_inc(s["sum_ready"], 1)
            dve.wait_ge(s["sum_ready"], k + 1)
            for j in range(2):
                src = windows(summed[:, par, j * N:(j + 1) * N])
                dst = mixed[:, bass.ds(k * CHUNK + j * N, N)].rearrange("p (a r b c) -> p a r b c", a=4, r=SS, b=4)
                blocks, order = (slice(1, 4, 2), slice(0, 3, 2)), (slice(None), slice(None, None, -1))
                for top in range(2):
                    for left in range(2):
                        rows, cs = slice(top * SS, top * SS + SS), slice(left * SS, left * SS + SS)
                        nc.vector.tensor_copy(
                            dst[:, blocks[top], :, blocks[left], :].rearrange("p a r b c -> p a b r c"),
                            src[:, order[top], order[left], rows, cs]).then_inc(s["mixed_ready"], 1)
            for j in range(2):
                dve.wait_ge(s["mixed_ready"], k * 2 * QUARTERS + (j + 1) * QUARTERS)
                nc.vector.bn_stats(stats[:, bass.ds(k * 2 + j, 1), :], mixed[:, bass.ds(k * CHUNK + j * N, N)]).then_inc(s["stats_ready"], 1)

        chunk_loop(dve, step)


def channel_attention(nc, ctx, sem, mixed, stats, ident, average, w, out):
    def sb(name, shape, dt=F32):
        return ctx.enter_context(nc.sbuf_tensor(name, shape, dt))

    def bank(name, count=1):
        return ctx.enter_context(nc.psum_tensor(name, [128, count, 512], F32))

    moments = sb("moments", [C, B, 2])
    mean2 = sb("mean2", [C, B, 2])
    mean = sb("mean", [C, B])
    spread2 = sb("spread2", [C, B, 2])
    log_var = sb("log_var3", [C, B])
    eps = sb("eps3", [C, 1])
    scaled_taps = sb("scaled_taps", [C, TAPS, C])
    turned_w = sb("turned_w", [C, 3, 4, C])
    recip_alpha = sb("recip_alpha", [C, 1])
    bias_pad = sb("bias_pad", [C, PADW, PADW])
    v_map = sb("v_map", [C, N])
    x_pad = sb("x_pad", [C, 2, PADW, PADW])
    q_pad = sb("q_pad", [C, 2, PADW, PADW])
    k_pad = sb("k_pad", [C, 2, PADW, PADW])
    moment = sb("moment", [C, 2])
    x_scaled = sb("x_scaled", [C, N])
    x_gained = sb("x_gained", [C, N])
    q_conv = sb("q_conv", [C, N])
    k_conv = sb("k_conv", [C, N])
    v_sb = sb("v_sb", [C, 2, N])
    tokens = sb("tokens", [128, 2, 2, C])
    logits = sb("logits", [C, C])
    peak = sb("peak3", [C, 1])
    neg_peak = sb("neg_peak", [C, 1])
    row_sum = sb("row_sum", [C, 1])
    recip_sum = sb("recip_sum", [C, 1])
    attn = sb("attn", [C, C])
    av_sb = sb("av_sb", [C, N])
    y_sb = sb("y_sb", [C, 2, N])

    ps_setup = bank("ps_setup3", 3)
    ps_qk = ps_setup[0:C, 0, :]
    ps_v = ps_setup[0:C, 1, 0:N]
    ps_tok = ps_setup[:, 2, 0:4 * C].rearrange("p (n k c) -> p n k c", n=2, k=2)
    ps_gram = bank("ps_gram")[0:C, 0, 0:C]
    ps_av = bank("ps_av")[0:C, 0, 0:N]
    ps_y = bank("ps_y3")[0:C, 0, 0:N]
    ps_moments = bank("ps_moments")[0:C, 0, 0:2 * B]

    turned = turned_w[:, :, :, :].rearrange("p a b c -> p (a b) c")
    point_q, point_k, final, v_taps = turned[:, 0, :], turned[:, 1, :], turned[:, 2, :], turned[:, 3:3 + TAPS, :]

    zeroed = sem("zeroed3")
    moments_set = sem("moments_set")
    moments_pe = sem("moments_pe")
    log_set = sem("log_set")
    rstd_set = sem("rstd_set")
    taps_scaled = sem("taps_scaled")
    weights_turned = sem("weights_turned")
    weights_copied = sem("weights_copied")
    map_steps = sem("map_steps")
    alpha_set = sem("alpha_set")
    out_done = [sem("out_done0"), sem("out_done1")]
    s = {n: sem(n + "_3") for n in (
        "moment_ready", "scaled", "gained", "normed", "x_padded", "qk_ready", "q_padded", "k_padded", "v_summed",
        "v_ready", "q_taps", "k_taps", "tok_ready", "tok_copied", "gram_ready", "logits_ready", "peak_ready",
        "neg_ready", "exp_ready", "recip_ready", "attn_ready", "av_ready", "av_copied", "final_ready", "y_ready")}

    def inside(padded):
        return padded[:, 1:H + 1, 1:W + 1]

    def tap(padded, k):
        return padded[:, k // 3:k // 3 + H, k % 3:k % 3 + W]

    def pads_zeroed(engine):
        engine.wait_ge(zeroed, 5)

    block = ctx.enter_context(nc.Block())

    @block.sync
    def _(sp):
        def step(t, half, par):
            sp.wait_ge(s["y_ready"], t + 1)
            dst = out[bass.ds(t, 1)].rearrange("a c h w -> c (a h w)")
            sp.dma_start(dst, y_sb[:, par, :]).then_inc(out_done[par], 16)

        image_loop(sp, step)
        for par in range(2):
            sp.wait_ge(out_done[par], 16 * (B // 2))

    @block.gpsimd
    def _(pool):
        nc.gpsimd.memset(eps[:, :], EPS).then_inc(zeroed, 1)
        for pad in (bias_pad[:, :, :], x_pad[:, :, :, :], q_pad[:, :, :, :], k_pad[:, :, :, :]):
            nc.gpsimd.memset(pad, 0.0).then_inc(zeroed, 1)


    @block.scalar
    def _(act):
        nc.scalar.preload_act_table_set("natural_log_exp_and_others")
        for b in range(3):
            act.wait_ge(weights_turned, 4 * (b + 1))
            nc.scalar.copy(turned_w[:, b, :, :], ps_setup[0:C, b, 0:4 * C].rearrange("p (k c) -> p k c", k=4)).then_inc(weights_copied, 1)
        pads_zeroed(act)
        act.wait_ge(moments_set, 7)
        nc.scalar.activation(log_var[:, :], spread2[:, :, 0], ACT.Ln, scale=0.5, bias=eps[:, 0:1]).then_inc(log_set, 1)
        act.wait_ge(log_set, 1)
        nc.scalar.activation(moments[:, :, 0], log_var[:, :], ACT.Exp, scale=-0.5).then_inc(rstd_set, 1)
        act.wait_ge(moments_set, 8)

        def scale(t):
            pads_zeroed(act)
            need(act, s["scaled"], t)
            nc.scalar.copy(moment[:, :], moments[:, bass.ds(t, 1), :].rearrange("p a b -> p (a b)")).then_inc(s["moment_ready"], 1)
            pads_zeroed(act)
            act.wait_ge(s["moment_ready"], t + 1)
            need(act, s["gained"], t)
            nc.scalar.activation(x_scaled[:, :], mixed[:, bass.ds(t * N, N)], ACT.Identity, bias=moment[:, 1:2],
                                 scale=moment[:, 0:1]).then_inc(s["scaled"], 1)

        def pad_x(t, par):
            pads_zeroed(act)
            act.wait_ge(s["normed"], t + 1)
            need(act, s["v_summed"], t - 1)
            nc.scalar.copy(inside(x_pad[:, par]), grid(mixed[:, bass.ds(t * N, N)])).then_inc(s["x_padded"], 1)

        def pad_q_k(t, par):
            act.wait_ge(s["qk_ready"], t + 1)
            need(act, s["q_taps"], (t - 1) * TAPS)
            nc.scalar.activation(inside(q_pad[:, par]), grid(ps_qk[:, 0:N]), ACT.Identity,
                                 bias=w["point_b"][:, 0:1]).then_inc(s["q_padded"], 1)
            need(act, s["k_taps"], (t - 1) * TAPS)
            nc.scalar.activation(inside(k_pad[:, par]), grid(ps_qk[:, N:2 * N]), ACT.Identity,
                                 bias=w["point_b"][:, 1:2]).then_inc(s["k_padded"], 1)

        def copy_tokens(t):
            act.wait_ge(s["tok_ready"], t + 1)
            need(act, s["gram_ready"], t)
            nc.scalar.copy(tokens[:, :, :, :], ps_tok).then_inc(s["tok_copied"], 1)

        def exponent(t):
            act.wait_ge(s["neg_ready"], t + 1)
            need(act, s["recip_ready"], t)
            nc.scalar.activation(logits[:, :], logits[:, :], ACT.Exp, bias=neg_peak[:, 0:1],
                                 accum_out=row_sum[:, 0:1]).then_inc(s["exp_ready"], 1)

        def copy_av(t):
            act.wait_ge(s["av_ready"], t + 1)
            need(act, s["final_ready"], t)
            nc.scalar.copy(av_sb[:, :], ps_av).then_inc(s["av_copied"], 1)

        scale(0)
        pad_x(0, 0)
        pad_q_k(0, 0)
        scale(1)

        def step(t, half, par):
            if not is_image(t, 0):
                copy_tokens(t - 1)
            if not is_image(t, B - 1):
                pad_x(t + 1, 1 - par)
                pad_q_k(t + 1, 1 - par)
            if not is_image(t, 0):
                exponent(t - 1)
                copy_av(t - 1)
            if not is_image(t, B - 1) and not is_image(t, B - 2):
                scale(t + 2)

        image_loop(act, step)
        copy_tokens(B - 1)
        exponent(B - 1)
        copy_av(B - 1)

    @block.vector
    def _(dve):
        for k in range(TAPS):
            nc.vector.tensor_scalar(scaled_taps[:, k, :], w["point_v"][:, :], w["taps"][:, 2, k:k + 1], None,
                                    ALU.mult).then_inc(taps_scaled, 1)
        means, deviations = stats[:, :, 1::3], stats[:, :, 2::3]
        dve.wait_ge(moments_pe, 1)
        nc.vector.tensor_copy(mean2[:, :, :], ps_moments.rearrange("p (t e) -> p t e", e=2)).then_inc(moments_set, 1)
        dve.wait_ge(moments_set, 1)
        nc.vector.tensor_tensor(mean[:, :], mean2[:, :, 0], mean2[:, :, 1], ALU.add).then_inc(moments_set, 1)
        dve.wait_ge(moments_set, 2)
        nc.vector.tensor_scalar(mean[:, :], mean[:, :], 0.5, None, ALU.mult).then_inc(moments_set, 1)
        dve.wait_ge(moments_set, 3)
        nc.vector.tensor_tensor(mean2[:, :, :], means, mean[:, :].unsqueeze(2).to_broadcast((C, B, 2)),
                                ALU.subtract).then_inc(moments_set, 1)
        dve.wait_ge(moments_set, 4)
        nc.vector.tensor_tensor(spread2[:, :, :], mean2[:, :, :], mean2[:, :, :], ALU.mult).then_inc(moments_set, 1)
        dve.wait_ge(moments_set, 5)
        nc.vector.scalar_tensor_tensor(out=spread2[:, :, :], in0=deviations, scalar=2.0 / N, in1=spread2[:, :, :],
                                       op0=ALU.mult, op1=ALU.add).then_inc(moments_set, 1)
        dve.wait_ge(moments_pe, 2)
        nc.vector.tensor_reduce(spread2[:, :, 0], ps_moments.rearrange("p (t e) -> p t e", e=2), AX_X,
                                ALU.add).then_inc(moments_set, 1)
        dve.wait_ge(rstd_set, 1)
        nc.vector.scalar_tensor_tensor(out=moments[:, :, 1], in0=mean[:, :], scalar=-1.0, in1=moments[:, :, 0],
                                       op0=ALU.mult, op1=ALU.mult).then_inc(moments_set, 1)
        nc.vector.reciprocal(recip_alpha[:, :], w["alpha"][:, :]).then_inc(alpha_set, 1)

        def affine(t):
            dve.wait_ge(s["scaled"], t + 1)
            need(dve, s["normed"], t)
            nc.vector.tensor_tensor(x_gained[:, :], x_scaled[:, :], w["ln_g"][:, :], ALU.mult).then_inc(s["gained"], 1)
            dve.wait_ge(s["gained"], t + 1)
            nc.vector.tensor_tensor(mixed[:, bass.ds(t * N, N)], x_gained[:, :], w["ln_b"][:, :],
                                    ALU.add).then_inc(s["normed"], 1)

        def conv_q(t, par, first, last):
            acc, pad = grid(q_conv[:, :]), q_pad[:, par]
            if first == 0:
                dve.wait_ge(s["q_padded"], t + 1)
                need(dve, s["tok_ready"], t)
                nc.vector.tensor_scalar(acc, tap(pad, 0), w["taps"][:, 0, 0:1], w["taps_b"][:, 0:1],
                                        ALU.mult, ALU.add).then_inc(s["q_taps"], 1)
            for k in range(max(first, 1), last + 1):
                dve.wait_ge(s["q_taps"], t * TAPS + k)
                nc.vector.scalar_tensor_tensor(out=acc, in0=tap(pad, k), scalar=w["taps"][:, 0, k:k + 1], in1=acc,
                                               op0=ALU.mult, op1=ALU.add).then_inc(s["q_taps"], 1)

        def conv_k(t, par):
            acc, pad = grid(k_conv[:, :]), k_pad[:, par]
            dve.wait_ge(s["k_padded"], t + 1)
            need(dve, s["tok_ready"], t)
            nc.vector.tensor_scalar(acc, tap(pad, 0), w["taps"][:, 1, 0:1], w["taps_b"][:, 1:2],
                                    ALU.mult, ALU.add).then_inc(s["k_taps"], 1)
            for k in range(1, TAPS):
                dve.wait_ge(s["k_taps"], t * TAPS + k)
                nc.vector.scalar_tensor_tensor(out=acc, in0=tap(pad, k), scalar=w["taps"][:, 1, k:k + 1], in1=acc,
                                               op0=ALU.mult, op1=ALU.add).then_inc(s["k_taps"], 1)

        def finish_v(t, par):
            dve.wait_ge(s["v_summed"], t + 1)
            need(dve, s["av_ready"], t - 1)
            nc.vector.tensor_tensor(v_sb[:, par, :], ps_v, v_map[:, :], ALU.add).then_inc(s["v_ready"], 1)

        def make_logits(t):
            dve.wait_ge(s["gram_ready"], t + 1)
            need(dve, s["attn_ready"], t)
            nc.vector.scalar_tensor_tensor(out=logits[:, :], in0=ps_gram, scalar=recip_alpha[:, 0:1],
                                           in1=w["block_mask"][:, :], op0=ALU.mult, op1=ALU.add).then_inc(s["logits_ready"], 1)
            dve.wait_ge(s["logits_ready"], t + 1)
            need(dve, s["neg_ready"], t)
            nc.vector.tensor_reduce(peak[:, :], logits[:, :], AX_X, ALU.max).then_inc(s["peak_ready"], 1)
            dve.wait_ge(s["peak_ready"], t + 1)
            need(dve, s["exp_ready"], t)
            nc.vector.tensor_scalar(neg_peak[:, :], peak[:, :], -1.0, None, ALU.mult).then_inc(s["neg_ready"], 1)

        def normalise(t):
            dve.wait_ge(s["exp_ready"], t + 1)
            nc.vector.reciprocal(recip_sum[:, :], row_sum[:, :]).then_inc(s["recip_ready"], 1)
            dve.wait_ge(s["recip_ready"], t + 1)
            need(dve, s["av_ready"], t)
            nc.vector.tensor_scalar(attn[:, :], logits[:, :], recip_sum[:, 0:1], None, ALU.mult).then_inc(s["attn_ready"], 1)

        def finish(t, half, par):
            dve.wait_ge(s["final_ready"], t + 1)
            need(dve, out_done[par], half * 16)
            nc.vector.scalar_tensor_tensor(out=y_sb[:, par, :], in0=ps_y, scalar=w["final_b"][:, 0:1],
                                           in1=mixed[:, bass.ds(t * N, N)], op0=ALU.add, op1=ALU.add).then_inc(s["y_ready"], 1)

        affine(0)
        dve.wait_ge(zeroed, 5)
        nc.vector.tensor_scalar(inside(bias_pad[:, :, :]), inside(bias_pad[:, :, :]), w["point_b"][:, 2:3], None,
                                ALU.add).then_inc(map_steps, 1)
        dve.wait_ge(map_steps, 1)
        nc.vector.tensor_scalar(grid(v_map[:, :]), tap(bias_pad, 0), w["taps"][:, 2, 0:1], w["taps_b"][:, 2:3],
                                ALU.mult, ALU.add).then_inc(map_steps, 1)
        for k in range(1, TAPS):
            dve.wait_ge(map_steps, k + 1)
            nc.vector.scalar_tensor_tensor(out=grid(v_map[:, :]), in0=tap(bias_pad, k), scalar=w["taps"][:, 2, k:k + 1],
                                           in1=grid(v_map[:, :]), op0=ALU.mult, op1=ALU.add).then_inc(map_steps, 1)
        dve.wait_ge(map_steps, TAPS + 1)
        finish_v(0, 0)
        dve.wait_ge(alpha_set, 1)

        def step(t, half, par):
            if not is_image(t, B - 1):
                affine(t + 1)
            conv_q(t, par, 0, 3)
            if not is_image(t, 0):
                make_logits(t - 1)
            conv_q(t, par, 4, 6)
            if not is_image(t, 0):
                normalise(t - 1)
            conv_q(t, par, 7, 8)
            conv_k(t, par)
            if not is_image(t, B - 1):
                finish_v(t + 1, 1 - par)
            if not is_image(t, 0):
                finish(t - 1, half if par else half - 1, 1 - par)

        image_loop(dve, step)
        make_logits(B - 1)
        normalise(B - 1)
        finish(B - 1, B // 2 - 1, 1)

    @block.tensor
    def _(pe):
        for k in range(3 + TAPS):
            if k >= 3:
                pe.wait_ge(taps_scaled, k - 2)
            src = (w["point_q"], w["point_k"], w["final"])[k][:, :] if k < 3 else scaled_taps[:, k - 3, :]
            nc.tensor.transpose(ps_setup[0:C, k // 4, (k % 4) * C:(k % 4 + 1) * C], src,
                                ident[0:C, 0:C]).then_inc(weights_turned, 1)
        nc.tensor.matmul(ps_moments, average[:, :], stats[:, :, 1::3], start=True, stop=True).then_inc(moments_pe, 1)
        pe.wait_ge(moments_set, 6)
        nc.tensor.matmul(ps_moments, average[:, :], spread2[:, :, :], start=True, stop=True).then_inc(moments_pe, 1)
        pe.wait_ge(weights_copied, 3)

        def points(t, par):
            pe.wait_ge(s["x_padded"], t + 1)
            need(pe, s["k_padded"], t)
            need(pe, s["q_padded"], t)
            nc.tensor.matmul(ps_qk[:, 0:N], point_q, inside(x_pad[:, par]), start=True, stop=True)
            nc.tensor.matmul(ps_qk[:, N:2 * N], point_k, inside(x_pad[:, par]), start=True, stop=True,
                             skip_group_check=True).then_inc(s["qk_ready"], 1)

        def sum_v(t, par, first, last):
            if first == 0:
                need(pe, s["v_ready"], t)
            for k in range(first, last + 1):
                mm = nc.tensor.matmul(ps_v, v_taps[:, k, :], tap(x_pad[:, par], k), start=(k == 0),
                                      stop=(k == TAPS - 1))
            if last == TAPS - 1:
                mm.then_inc(s["v_summed"], 1)

        def turn_tokens(t):
            pe.wait_ge(s["q_taps"], (t + 1) * TAPS)
            pe.wait_ge(s["k_taps"], (t + 1) * TAPS)
            need(pe, s["tok_copied"], t)
            for n in range(2):
                for k, conv in enumerate((q_conv, k_conv)):
                    mm = nc.tensor.transpose(ps_tok[:, n, k, :], conv[:, n * 128:(n + 1) * 128], ident[0:C, 0:C])
            mm.then_inc(s["tok_ready"], 1)

        def gram(t):
            pe.wait_ge(s["tok_copied"], t + 1)
            need(pe, s["logits_ready"], t)
            for n in range(2):
                mm = nc.tensor.matmul(ps_gram, tokens[:, n, 1, :], tokens[:, n, 0, :], start=(n == 0), stop=(n == 1))
            mm.then_inc(s["gram_ready"], 1)

        def attend(t, par):
            pe.wait_ge(s["attn_ready"], t + 1)
            pe.wait_ge(s["v_ready"], t + 1)
            need(pe, s["av_copied"], t)
            nc.tensor.matmul(ps_av, attn[:, :], v_sb[:, par, :], start=True, stop=True).then_inc(s["av_ready"], 1)

        def finalise(t):
            pe.wait_ge(s["av_copied"], t + 1)
            need(pe, s["y_ready"], t)
            nc.tensor.matmul(ps_y, final, av_sb[:, :], start=True, stop=True).then_inc(s["final_ready"], 1)

        points(0, 0)
        sum_v(0, 0, 0, TAPS - 1)

        def step(t, half, par):
            if not is_image(t, 0):
                turn_tokens(t - 1)
            if not is_image(t, B - 1):
                points(t + 1, 1 - par)
            if not is_image(t, 0):
                gram(t - 1)
            if not is_image(t, B - 1):
                sum_v(t + 1, 1 - par, 0, 5)
            if not is_image(t, 0):
                attend(t - 1, 1 - par)
            if not is_image(t, B - 1):
                sum_v(t + 1, 1 - par, 6, TAPS - 1)
            if not is_image(t, 0):
                finalise(t - 1)

        image_loop(pe, step)
        turn_tokens(B - 1)
        gram(B - 1)
        attend(B - 1, 1)
        finalise(B - 1)


_INS = ['x', 'L0_conv_qkv_w', 'L0_conv_qkv_b', 'L0_conv_proj_w', 'L0_conv_proj_b', 'L0_conv_rel_bias',
        'L0_conv_norm1_g', 'L0_conv_norm1_b', 'L0_conv_norm2_g', 'L0_conv_norm2_b', 'L0_conv_fc1_w',
        'L0_conv_fc1_b', 'L0_conv_fc2_w', 'L0_conv_fc2_b', 'L1_conv_ln_g', 'L1_conv_ln_b', 'L1_conv_wq_p',
        'L1_conv_bq_p', 'L1_conv_wq_d', 'L1_conv_bq_d', 'L1_conv_wk_p', 'L1_conv_bk_p', 'L1_conv_wk_d',
        'L1_conv_bk_d', 'L1_conv_wv_p', 'L1_conv_bv_p', 'L1_conv_wv_d', 'L1_conv_bv_d', 'L1_conv_alpha',
        'L1_conv_w_f', 'L1_conv_b_f']


def constants():
    f = np.float32
    head_mask = np.zeros((C, GROUP), f)
    for c in range(C):
        head_mask[c, (c // HD) % GROUP] = 1
    region = np.repeat([0, 1, 2], [H - WS, WS - SS, SS])
    label = region[:, None] * 3 + region[None, :]
    shift = np.zeros((2, WN, PAIRS, WN), f)
    for p in range(PAIRS):
        for w in range(2):
            win = label[p * WS:(p + 1) * WS, w * WS:(w + 1) * WS].reshape(-1)
            shift[w, :, p, :] = np.where(win[:, None] != win[None, :], -10.0, 0.0)
    head = np.arange(C) // HC
    return {
        "c_ident": np.eye(128, dtype=f),
        "c_center": (np.eye(C) - 1.0 / C).astype(f),
        "c_average": np.full((C, C), 1.0 / C, f),
        "c_head_mask": head_mask,
        "c_shift_mask": shift.reshape(128, PAIRS, WN),
        "c_block_mask": np.where(head[:, None] == head[None, :], 0.0, BLOCKED).astype(f),
    }


def kernel(**inputs):
    import concourse.bacc as _bacc
    from concourse.bass_utils import run_bass_kernel_spmd as _run

    nc = _bacc.Bacc("TRN2", target_bir_lowering=False, num_devices=1)
    arrays, args = {}, {}
    given = {name: np.ascontiguousarray(inputs[name]) for name in _INS}
    for name, v in {**given, **constants()}.items():
        arrays[f"in_{name}"] = v
        args[name] = nc.dram_tensor(f"in_{name}", v.shape, mybir.dt.from_np(v.dtype), kind="ExternalInput").ap()
    args["out"] = nc.dram_tensor("out_0", (B, C, H, W), F32, kind="ExternalOutput").ap()
    build(nc, args)
    r = _run(nc, [arrays], core_ids=[0])
    return r.results[0]["out_0"]
```

```python
from contextlib import ExitStack

import numpy as np

import concourse.bass as bass
from concourse import mybir

ALU = mybir.AluOpType
ACT = mybir.ActivationFunctionType
AX_X = mybir.AxisListType.X
F32 = mybir.dt.float32

B, C, H, W = 32, 96, 16, 16
N = H * W
HEADS, HD = 12, 8
WS, SS = 8, 4
WN = WS * WS
GROUP = 4
NG = HEADS // GROUP
PAIRS = 2
HP = HEADS // 2
SC = HEADS * WN
VC = HD + 1
HID = 4 * C
HT = HID // 128
REL = 2 * WS - 1
NH2, HC = 8, 12
SET_HEADS = 3
SET = SET_HEADS * HC
SETS = -(-NH2 // SET_HEADS)
EPS = 1e-5
SCALE = HD ** -0.5
PADW = W + 2
SIDE = 3
TAPS = SIDE * SIDE
STACK = SIDE * SET + SIDE + 1
ROWS = H * PADW
CHUNK = 2 * N
BLOCKED = -1e30


def need(engine, semaphore, count):
    if isinstance(count, int) and count <= 0:
        return
    engine.wait_ge(semaphore, count)


def led_image_loop(engine, step, tail=1, between=None):
    step(-2, -1, 0)
    if between:
        between()
    step(-1, -1, 1)
    image_loop(engine, step, tail)


def image_loop(engine, step, tail=1, lead=1, between=None, start=0):
    for half in range(lead):
        for par in range(2):
            if half * 2 + par >= start:
                step(half * 2 + par, half, par)
        if between:
            between(half)
    with engine.Fori(lead, B // 2 - tail) as i:
        step(i * 2, i, 0)
        step(i * 2 + 1, i, 1)
    for half in range(B // 2 - tail, B // 2):
        step(half * 2, half, 0)
        step(half * 2 + 1, half, 1)


def real(t):
    return not isinstance(t, int) or 0 <= t < B


def past(t):
    return isinstance(t, int) and t >= B


def is_image(t, other):
    return isinstance(t, int) and t == other


def build(nc, a, debug=None):
    ctx = ExitStack()
    with ctx:
        def sb(name, shape, dt=F32):
            return ctx.enter_context(nc.sbuf_tensor(name, shape, dt))

        def sem(name):
            return ctx.enter_context(nc.semaphore(name))

        stream = sb("stream", [C, B * N])
        ident = sb("ident", [128, 128])
        center = sb("center", [C, C])
        average = sb("average", [C, C])
        w = {name: sb(name, shape) for name, shape in (
            ("fc1", [C, HID]), ("fc2", [128, HT, C]), ("fc1_b", [128, HT]), ("fc2_b", [C, 1]),
            ("norm2_g", [C, 1]), ("norm2_b", [C, 1]),
            ("ln_g", [C, N]), ("ln_b", [C, N]),
            ("point", [3 * SET, SETS, SET]), ("point_b", [3 * SET, SETS]),
            ("taps", [3 * SET, SETS, TAPS]), ("taps_b", [3 * SET, SETS]),
            ("final", [C, C]), ("final_b", [C, 1]), ("alpha", [C, 1]),
            ("block_mask", [C, C]))}
        weights_in = sem("weights_in")
        zeroed_points = sem("zeroed_points")
        with ExitStack() as p1:
            window_attention(nc, p1, a, sem, stream, ident, center, average, w, weights_in, zeroed_points)
        if debug == 1:
            dump(nc, sem, stream, a["out"])
            return
        mixed = sb("mixed", [C, B * N])
        stats = sb("stats", [C, B, 6])
        with ExitStack() as p2:
            mlp(nc, p2, sem, stream, mixed, stats, center, average, w)
        if debug == 2:
            dump(nc, sem, mixed, a["out"])
            return
        with ExitStack() as p3:
            channel_attention(nc, p3, sem, mixed, stats, ident, average, w, a["c_stack_ones"], a["out"])


def dump(nc, sem, stream, out):
    done = sem("dumped")
    with nc.Block() as block:
        @block.sync
        def _(sp):
            for t in range(B):
                sp.dma_start(out[t].rearrange("c h w -> c (h w)"), stream[:, t * N:(t + 1) * N]).then_inc(done, 16)
            sp.wait_ge(done, 16 * B)


def grid(ap, width=W):
    return ap.rearrange("p (r c) -> p r c", c=width)


def windows(ap):
    return ap.rearrange("p (a w r c) -> p a w r c", a=2, w=2, r=WS)


def weight_loads(a, w):
    def column(name, k=0, n=C):
        return a[name][k * n:(k + 1) * n].rearrange("(c a) -> c a", a=1)

    loads = [
        (w["fc1"][:, :], a["L0_conv_fc1_w"]),
        (w["fc2"][:, :, :], a["L0_conv_fc2_w"].rearrange("(k p) c -> p k c", p=128)),
        (w["fc2_b"][:, :], column("L0_conv_fc2_b")),
        (w["norm2_g"][:, :], column("L0_conv_norm2_g")),
        (w["norm2_b"][:, :], column("L0_conv_norm2_b")),
        (w["ln_g"][:, :], a["L1_conv_ln_g"].rearrange("c h w -> c (h w)")),
        (w["ln_b"][:, :], a["L1_conv_ln_b"].rearrange("c h w -> c (h w)")),
        (w["final"][:, :], a["L1_conv_w_f"]),
        (w["final_b"][:, :], column("L1_conv_b_f")),
        (w["block_mask"][:, :], a["c_block_mask"]),
    ]
    loads += [(w["fc1_b"][:, k:k + 1], column("L0_conv_fc1_b", k, 128)) for k in range(HT)]
    for k, n in enumerate("qkv"):
        for j in range(SET_HEADS):
            at = slice(j * HC, (j + 1) * HC)
            heads = a[f"L1_conv_w{n}_p"][j::SET_HEADS]
            loads.append((w["point"][k * SET + j * HC:k * SET + (j + 1) * HC, 0:heads.shape[0], at],
                          heads.rearrange("s o c -> o s c")))
        for name, flat in (("point_b", a[f"L1_conv_b{n}_p"].rearrange("h (c a) -> (h c) a", a=1)),
                           ("taps", a[f"L1_conv_w{n}_d"].rearrange("c a i j -> c (a i j)")),
                           ("taps_b", a[f"L1_conv_b{n}_d"].rearrange("(c a) -> c a", a=1))):
            for g in range(SETS):
                count = min(SET, C - g * SET)
                loads.append((w[name][k * SET:k * SET + count, g] if name == "taps" else
                              w[name][k * SET:k * SET + count, g:g + 1], flat[g * SET:g * SET + count]))
    loads += [(w["alpha"][h * HC:(h + 1) * HC, :],
               a["L1_conv_alpha"][h:h + 1].rearrange("(b a) -> b a", a=1).to_broadcast((HC, 1))) for h in range(NH2)]
    return loads


def window_attention(nc, ctx, a, sem, stream, ident, center, average, w_late, weights_in, zeroed_points):
    def sb(name, shape, dt=F32):
        return ctx.enter_context(nc.sbuf_tensor(name, shape, dt))

    def bank(name, count=1):
        return ctx.enter_context(nc.psum_tensor(name, [128, count, 512], F32))

    head_mask = sb("head_mask", [C, GROUP])
    shift_mask = sb("shift_mask", [128, PAIRS, WN])
    rel_rows = sb("rel_rows", [128, WN, HEADS])
    bias = sb("bias", [128, PAIRS, SC])
    w_in = sb("w_in", [C, 3 * C])
    w_qkv = sb("w_qkv", [C, 3 * C])
    w_proj = sb("w_proj", [C, C])
    cols = sb("cols", [C, 7])
    b_q = sb("b_q", [C, 1])
    b_k = sb("b_k", [C, 1])
    b_v = sb("b_v", [C, 1])
    b_proj = sb("b_proj", [C, 1])
    x_in = sb("x_in", [C, 2, N])
    squares = sb("squares", [C, N])
    log_var = sb("log_var", [C, N])
    eps = sb("eps", [C, 1])
    rstd = sb("rstd", [C, N])
    normed = sb("normed", [C, 2 * PAIRS, 2, WN])
    q_sb = sb("q_sb", [C, N])
    k_blocks = sb("k_blocks", [C, GROUP, N])
    v_blocks = sb("v_blocks", [128, 2, PAIRS, HP + 2, 2, 2, VC])
    scores = sb("scores", [128, PAIRS, SC])
    peak = sb("peak", [128, PAIRS, HEADS])
    probs_t = sb("probs_t", [128, SC])
    recip = sb("recip", [128, HEADS])
    heads_out = sb("heads_out", [128, C])
    out_t = sb("out_t", [C, 2, N])

    ps_scores = bank("ps_scores", NG)
    ps_probs = bank("ps_probs", 2)
    ps_out = bank("ps_out")
    ps_a = bank("ps_a")
    ps_b = bank("ps_b")
    centred = ps_a[0:C, 0, 0:N]
    ps_var = ps_a[0:C, 0, N:2 * N]
    ps_k = ps_a[0:C, 0, 0:N]
    ps_q = ps_probs[0:C, 1, 512 - N:512]
    ps_v = ps_b[:, 0, 0:2 * PAIRS * C].rearrange("p (w c) -> p w c", c=C)
    ps_proj = ps_b[0:C, 0, 0:N]
    ps_pv = ps_out[:, 0, 0:HP * 4 * VC].rearrange("p (q w e c) -> p q w e c", q=HP, w=2, e=2)
    ps_ot = ps_out[0:C, 0, 384:512]

    consts_in = sem("consts_in")
    second_in = sem("second_in")
    rel_in = sem("rel_in")
    set_up = sem("set_up")
    pe_set = sem("pe_set")
    zeroed = sem("zeroed")
    x_landed = [sem("x_landed0"), sem("x_landed1")]
    s = {n: sem(n) for n in (
        "rolled", "centred_ready", "squares_ready", "var_ready", "log_ready", "rstd_ready", "normed_ready",
        "q_ready", "k_ready", "q_copied", "k_copied", "v_ready", "v_copied",
        "scores_ready", "biased", "peak_ready", "shifted", "probs_ready", "turned", "turned_copied",
        "pv_ready", "recip_ready", "heads_ready", "ot_ready", "ot_copied", "proj_ready", "residual_done")}

    FIRST, SECOND = 9, 4
    LEAD = 3

    x = a["x"]
    block = ctx.enter_context(nc.Block())

    @block.sync
    def _(sp):
        def column(name):
            return a[name].rearrange("(c a) -> c a", a=1)

        first = ((center[:, :], a["c_center"]), (average[:, :], a["c_average"]), (w_in[:, :], a["L0_conv_qkv_w"]),
                 (cols[:, 0:1], column("L0_conv_norm1_g")), (cols[:, 1:2], column("L0_conv_norm1_b")),
                 *((cols[:, 2 + k:3 + k], a["L0_conv_qkv_b"][k * C:(k + 1) * C].rearrange("(c a) -> c a", a=1))
                   for k in range(3)),
                 (head_mask[:, :], a["c_head_mask"]))
        second = ((shift_mask[:, :, :], a["c_shift_mask"]), (ident[:, :], a["c_ident"]),
                  (w_proj[:, :], a["L0_conv_proj_w"]), (cols[:, 5:6], column("L0_conv_proj_b")))
        assert (len(first), len(second)) == (FIRST, SECOND)
        late = weight_loads(a, w_late)

        def step(t, half, par):
            need(sp, s["rolled"], (t - 1) * 3)
            xt = x[bass.ds(t, 1)] if not isinstance(t, int) else x[t:t + 1]
            xt = xt.rearrange("a c h w -> c (a h w)")
            sp.dma_start(x_in[:, par, 0:N - SS * W], xt[:, SS * W:N]).then_inc(x_landed[par], 16)
            sp.dma_start(x_in[:, par, N - SS * W:N], xt[:, 0:SS * W]).then_inc(x_landed[par], 16)

        def after_pair(half):
            if half == 0:
                sp.wait_ge(zeroed_points, 4)
            for dst, src in late[half::LEAD]:
                sp.dma_start(dst, src).then_inc(weights_in, 16)

        for dst, src in first:
            sp.dma_start(dst, src).then_inc(consts_in, 16)
        step(0, 0, 0)
        step(1, 0, 1)
        for dst, src in second:
            sp.dma_start(dst, src).then_inc(second_in, 16)
        table = a["L0_conv_rel_bias"]
        for upper in range(2):
            for y in range(WS):
                runs = bass.AP(table.tensor, y * REL * HEADS, [[HEADS, WS], [REL * HEADS, WS], [1, WS * HEADS]])
                at = upper * WN + y * WS
                sp.dma_start(rel_rows[at:at + WS, :, :].rearrange("p (r c) h -> p r (c h)", r=WS),
                             runs).then_inc(rel_in, 16)
        image_loop(sp, step, lead=LEAD, between=after_pair, start=2)
        sp.wait_ge(weights_in, 16 * len(late))

    @block.gpsimd
    def _(pool):
        nc.gpsimd.memset(w_late["point"][:, :, :], 0.0).then_inc(zeroed_points, 1)
        nc.gpsimd.memset(w_late["taps"][:, :, :], 0.0).then_inc(zeroed_points, 1)
        nc.gpsimd.memset(w_late["point_b"][:, :], 0.0).then_inc(zeroed_points, 1)
        nc.gpsimd.memset(w_late["taps_b"][:, :], 0.0).then_inc(zeroed_points, 1)
        nc.gpsimd.memset(v_blocks[:, :, :, :, :, :, :], 0.0).then_inc(zeroed, 1)
        nc.gpsimd.memset(eps[:, :], EPS).then_inc(zeroed, 1)
        pool.wait_ge(zeroed, 2)
        for e in range(2):
            for par in range(2):
                nc.gpsimd.memset(v_blocks[64 * e:64 * e + 64, par, :, :, :, e, HD:VC], 1.0).then_inc(zeroed, 1)

        def subtract_peak(t, p):
            u = t * 2 + p
            pool.wait_ge(s["peak_ready"], u + 1)
            sc = scores[:, p, :].rearrange("p (h m) -> p h m", m=WN)
            nc.gpsimd.tensor_tensor(sc, sc, peak[:, p, :].unsqueeze(2).to_broadcast((128, HEADS, WN)),
                                    ALU.subtract).then_inc(s["shifted"], 1)

        def step(t, half, par):
            subtract_peak(t, 0)
            subtract_peak(t, 1)

        image_loop(pool, step)

    @block.scalar
    def _(act):
        def square(t):
            act.wait_ge(s["centred_ready"], t + 1)
            need(act, s["var_ready"], t)
            nc.scalar.activation(squares[:, :], centred, ACT.Square).then_inc(s["squares_ready"], 1)

        def inverse_deviation(t):
            act.wait_ge(s["var_ready"], t + 1)
            need(act, s["rstd_ready"], t)
            nc.scalar.activation(log_var[:, :], ps_var, ACT.Ln, bias=eps[:, 0:1]).then_inc(s["log_ready"], 1)
            act.wait_ge(s["log_ready"], t + 1)
            need(act, s["normed_ready"], t)
            nc.scalar.activation(rstd[:, :], log_var[:, :], ACT.Exp, scale=-0.5).then_inc(s["rstd_ready"], 1)

        def copy_q(t):
            act.wait_ge(s["q_ready"], t + 1)
            need(act, s["scores_ready"], t * 2)
            nc.scalar.activation(q_sb[:, :], ps_q, ACT.Identity, bias=b_q[:, 0:1], scale=SCALE).then_inc(s["q_copied"], 1)

        def copy_v(t, par):
            act.wait_ge(s["v_ready"], t + 1)
            need(act, s["pv_ready"], (t - 1) * 2)
            for e in range(2):
                src = ps_v[64 * e:64 * e + 64].rearrange("p w (q e d) -> p w q e d", q=HP, e=2)
                for p in range(PAIRS):
                    nc.scalar.copy(v_blocks[64 * e:64 * e + 64, par, p, 0:HP, :, e, 0:HD],
                                   src[:, 2 * p:2 * p + 2, :, e, :].rearrange("p w q d -> p q w d")).then_inc(s["v_copied"], 1)

        def exponent(t, p):
            act.wait_ge(s["shifted"], t * 2 + p + 1)
            nc.scalar.activation(scores[:, p, :], scores[:, p, :], ACT.Exp).then_inc(s["probs_ready"], 1)

        def copy_turned(t, p):
            u = t * 2 + p
            act.wait_ge(s["turned"], u + 1)
            need(act, s["pv_ready"], u)
            nc.scalar.copy(probs_t[:, :], ps_probs[:, :, :].rearrange("p k c -> p (k c)")[:, 0:SC]).then_inc(s["turned_copied"], 1)

        def copy_ot(t, p, par):
            act.wait_ge(s["ot_ready"], t * 2 + p + 1)
            need(act, s["proj_ready"], t - 1)
            nc.scalar.copy(out_t[:, par, p * 2 * WN:(p + 1) * 2 * WN], ps_ot).then_inc(s["ot_copied"], 1)

        nc.scalar.preload_act_table_set("natural_log_exp_and_others")
        act.wait_ge(zeroed, 6)
        act.wait_ge(set_up, 5)

        def step(t, half, par):
            if real(t):
                copy_ot(t, 0, par)
            if real(t + 2):
                square(t + 2)
            if real(t):
                copy_turned(t, 1)
            if real(t + 2):
                inverse_deviation(t + 2)
            if real(t + 1):
                exponent(t + 1, 0)
            if real(t):
                copy_ot(t, 1, par)
            if real(t + 2):
                copy_q(t + 2)
            if real(t + 1):
                copy_turned(t + 1, 0)
            if real(t + 2):
                copy_v(t + 2, par)
            if real(t + 1):
                exponent(t + 1, 1)

        led_image_loop(act, step)

    @block.vector
    def _(dve):
        dve.wait_ge(consts_in, 16 * FIRST)
        nc.vector.tensor_scalar(w_qkv[:, :], w_in[:, :], cols[:, 0:1], None, ALU.mult).then_inc(set_up, 1)
        dve.wait_ge(pe_set, 3)
        nc.vector.tensor_tensor(b_q[:, :], ps_a[0:C, 0, 0:1], cols[:, 2:3], ALU.add).then_inc(set_up, 1)
        nc.vector.tensor_tensor(b_k[:, :], ps_a[0:C, 0, 1:2], cols[:, 3:4], ALU.add).then_inc(set_up, 1)
        nc.vector.tensor_tensor(b_v[:, :], ps_a[0:C, 0, 2:3], cols[:, 4:5], ALU.add).then_inc(set_up, 1)
        dve.wait_ge(set_up, 3)
        nc.vector.tensor_scalar(b_q[:, :], b_q[:, :], SCALE, None, ALU.mult).then_inc(set_up, 1)

        def set_up_rest():
            dve.wait_ge(second_in, 16 * SECOND)
            dve.wait_ge(rel_in, 16 * 2 * WS)
            for p in range(PAIRS):
                nc.vector.tensor_tensor(bias[:, p, :].rearrange("p (h m) -> p h m", m=WN),
                                        rel_rows[:, ::-1, :].rearrange("p m h -> p h m"),
                                        shift_mask[:, p, :].unsqueeze(1).to_broadcast((128, HEADS, WN)),
                                        ALU.add).then_inc(set_up, 1)
            dve.wait_ge(pe_set, 4)
            nc.vector.tensor_tensor(b_proj[:, :], ps_out[0:C, 0, 0:1], cols[:, 5:6], ALU.add).then_inc(set_up, 1)
            dve.wait_ge(set_up, 8)

        def roll(t, half, par):
            dve.wait_ge(x_landed[par], (half + 1) * 32)
            src = grid(x_in[:, par, :])
            dst = windows(stream[:, bass.ds(t * N, N)])
            for w, c0, n, at in ((0, 0, WS, SS), (1, 0, SS, WS + SS), (1, SS, SS, 0)):
                nc.vector.tensor_copy(dst[:, :, w, :, c0:c0 + n],
                                      src[:, :, at:at + n].rearrange("p (a r) c -> p a r c", a=2)).then_inc(s["rolled"], 1)

        def normalise(t):
            dve.wait_ge(s["rstd_ready"], t + 1)
            need(dve, s["v_ready"], t)
            def twice(ap):
                return ap.rearrange("p (w m) -> p w m", m=WN).unsqueeze(2).to_broadcast((C, 2 * PAIRS, 2, WN))
            nc.vector.tensor_tensor(normed[:, :, :, :], twice(centred), twice(rstd[:, :]),
                                    ALU.mult).then_inc(s["normed_ready"], 1)

        def copy_k(t):
            dve.wait_ge(s["k_ready"], t + 1)
            need(dve, s["scores_ready"], t * 2)
            for j in range(GROUP):
                nc.vector.tensor_scalar(k_blocks[:, j, :], ps_k, b_k[:, 0:1], head_mask[:, j:j + 1],
                                        ALU.add, ALU.mult).then_inc(s["k_copied"], 1)

        def add_bias(t, p):
            u = t * 2 + p
            dve.wait_ge(s["scores_ready"], u + 1)
            need(dve, s["turned"], u - 1)
            nc.vector.tensor_tensor(scores[:, p, :].rearrange("p (g c) -> p g c", g=NG),
                                    ps_scores[:, :, 0:GROUP * WN],
                                    bias[:, p, :].rearrange("p (g c) -> p g c", g=NG), ALU.add).then_inc(s["biased"], 1)
            dve.wait_ge(s["biased"], u + 1)
            need(dve, s["shifted"], u - 1)
            nc.vector.tensor_reduce(peak[:, p, :], scores[:, p, :].rearrange("p (h m) -> p h m", m=WN),
                                    AX_X, ALU.max).then_inc(s["peak_ready"], 1)

        def weigh_heads(t, p):
            u = t * 2 + p
            dve.wait_ge(s["pv_ready"], u + 1)
            need(dve, s["heads_ready"], u * 2)
            for w in range(2):
                rows = slice(64 * w, 64 * w + 64)
                nc.vector.reciprocal(recip[rows, :].rearrange("p (q e) -> p q e", e=2),
                                     ps_pv[rows, :, w, :, HD]).then_inc(s["recip_ready"], 1)
            dve.wait_ge(s["recip_ready"], (u + 1) * 2)
            need(dve, s["ot_ready"], u)
            for w in range(2):
                rows = slice(64 * w, 64 * w + 64)
                r = recip[rows, :].rearrange("p (q e) -> p q e", e=2).unsqueeze(3).to_broadcast((64, HP, 2, HD))
                nc.vector.tensor_tensor(heads_out[rows, :].rearrange("p (q e d) -> p q e d", q=HP, e=2),
                                        ps_pv[rows, :, w, :, 0:HD], r, ALU.mult).then_inc(s["heads_ready"], 1)

        def add_residual(t):
            dve.wait_ge(s["proj_ready"], t + 1)
            dst = stream[:, bass.ds(t * N, N)]
            nc.vector.scalar_tensor_tensor(out=dst, in0=ps_proj, scalar=b_proj[:, 0:1], in1=dst,
                                           op0=ALU.add, op1=ALU.add).then_inc(s["residual_done"], 1)

        def step(t, half, par):
            if real(t + 1):
                add_bias(t + 1, 0)
            if real(t - 1):
                add_residual(t - 1)
            if real(t + 3):
                roll(t + 3, half + 1 + par, 1 - par)
            if real(t + 2):
                normalise(t + 2)
            if real(t):
                weigh_heads(t, 1)
            if real(t + 1):
                add_bias(t + 1, 1)
            if real(t + 2):
                copy_k(t + 2)
            if real(t + 1):
                weigh_heads(t + 1, 0)

        roll(0, 0, 0)
        led_image_loop(dve, step, tail=2, between=set_up_rest)
        add_residual(B - 1)

    @block.tensor
    def _(pe):
        pe.wait_ge(consts_in, 16 * FIRST)
        for k in range(3):
            nc.tensor.matmul(ps_a[0:C, 0, k:k + 1], w_in[:, k * C:(k + 1) * C], cols[:, 1:2],
                             start=True, stop=True, skip_group_check=True).then_inc(pe_set, 1)
        pe.wait_ge(set_up, 4)

        def fold_v():
            pe.wait_ge(second_in, 16 * SECOND)
            nc.tensor.matmul(ps_out[0:C, 0, 0:1], w_proj[:, :], b_v[:, 0:1], start=True, stop=True).then_inc(pe_set, 1)
            pe.wait_ge(set_up, 8)

        def centre(t):
            pe.wait_ge(s["rolled"], (t + 1) * 3)
            need(pe, s["k_copied"], t * GROUP)
            nc.tensor.matmul(centred, center[:, :], stream[:, bass.ds(t * N, N)],
                             start=True, stop=True).then_inc(s["centred_ready"], 1)

        def spread(t):
            pe.wait_ge(s["squares_ready"], t + 1)
            nc.tensor.matmul(ps_var, average[:, :], squares[:, :], start=True, stop=True).then_inc(s["var_ready"], 1)

        def make_q_k(t):
            pe.wait_ge(s["normed_ready"], t + 1)
            need(pe, s["turned_copied"], (t - 1) * 2)
            nc.tensor.matmul(ps_q, w_qkv[:, 0:C], normed[:, :, 0, :], start=True, stop=True,
                             skip_group_check=True).then_inc(s["q_ready"], 1)
            nc.tensor.matmul(ps_k, w_qkv[:, C:2 * C], normed[:, :, 0, :], start=True, stop=True).then_inc(s["k_ready"], 1)

        def make_v(t):
            pe.wait_ge(s["normed_ready"], t + 1)
            need(pe, s["residual_done"], t - 2)
            for w in range(2 * PAIRS):
                twice = normed[:, w, :, :].rearrange("p e m -> p (e m)")
                mm = nc.tensor.matmul(ps_v[:, w, :], twice, w_qkv[:, 2 * C:3 * C], start=True, stop=True,
                                      skip_group_check=True)
            mm.then_inc(s["v_ready"], 1)

        def score(t, p):
            u = t * 2 + p
            pe.wait_ge(s["q_copied"], t + 1)
            pe.wait_ge(s["k_copied"], (t + 1) * GROUP)
            need(pe, s["biased"], u)
            for g in range(NG):
                ch = slice(32 * g, 32 * g + 32)
                for w in range(2):
                    tokens = slice((2 * p + w) * WN, (2 * p + w + 1) * WN)
                    q, k = q_sb[ch, tokens], k_blocks[ch, :, tokens]
                    mm = nc.tensor.matmul(ps_scores[64 * w:64 * w + 64, g, 0:GROUP * WN], q, k, start=True, stop=True)
            mm.then_inc(s["scores_ready"], 1)

        def turn(t, p):
            u = t * 2 + p
            pe.wait_ge(s["probs_ready"], u + 1)
            need(pe, s["turned_copied"], u)
            for q in range(HP):
                if q == 4:
                    pe.wait_ge(s["q_copied"], min(t + 2, B) if isinstance(t, int) else t + 2)
                mm = nc.tensor.transpose(ps_probs[:, q // 4, (q % 4) * 128:(q % 4 + 1) * 128],
                                         scores[:, p, q * 128:(q + 1) * 128], ident[:, :])
            mm.then_inc(s["turned"], 1)

        def weigh(t, p, par):
            u = t * 2 + p
            pe.wait_ge(s["turned_copied"], u + 1)
            pe.wait_ge(s["v_copied"], (t + 1) * 4)
            need(pe, s["ot_copied"], u)
            for q in range(HP):
                mm = nc.tensor.matmul(ps_out[:, 0, q * 4 * VC:(q + 3) * 4 * VC], probs_t[:, q * 128:(q + 1) * 128],
                                      v_blocks[:, par, p, q:q + 3, :, :, :].rearrange("p q w e c -> p (q w e c)"),
                                      start=True, stop=True, skip_group_check=True)
            mm.then_inc(s["pv_ready"], 1)

        def turn_heads(t, p):
            u = t * 2 + p
            pe.wait_ge(s["heads_ready"], (u + 1) * 2)
            nc.tensor.transpose(ps_ot, heads_out[:, :], ident[:, :]).then_inc(s["ot_ready"], 1)

        def project(t, par, vs):
            pe.wait_ge(s["ot_copied"], (t + 1) * 2)
            pe.wait_ge(s["v_copied"], vs * 4)
            nc.tensor.matmul(ps_proj, w_proj[:, :], out_t[:, par, :], start=True, stop=True).then_inc(s["proj_ready"], 1)

        def step(t, half, par):
            if real(t):
                turn_heads(t, 0)
            if real(t + 2):
                centre(t + 2)
            if real(t):
                turn(t, 1)
            if real(t - 1):
                project(t - 1, 1 - par, B if is_image(t, B - 1) else t + 2)
            if real(t + 2):
                spread(t + 2)
            if real(t):
                weigh(t, 1, par)
            if real(t + 1):
                score(t + 1, 1)
            if real(t):
                turn_heads(t, 1)
            if real(t + 2):
                make_q_k(t + 2)
            if real(t + 1):
                turn(t + 1, 0)
            if real(t + 2):
                make_v(t + 2)
            if real(t + 1):
                weigh(t + 1, 0, 1 - par)
            if real(t + 2):
                score(t + 2, 0)

        led_image_loop(pe, step, between=fold_v)
        project(B - 1, 1, B)


def chunk_loop(engine, step):
    n = B * N // CHUNK
    step(0, 0, 0)
    step(1, 0, 1)
    with engine.Fori(1, n // 2 - 1) as i:
        step(i * 2, i, 0)
        step(i * 2 + 1, i, 1)
    step(n - 2, n // 2 - 1, 0)
    step(n - 1, n // 2 - 1, 1)


def mlp(nc, ctx, sem, stream, mixed, stats, center, average, w):
    CHUNKS = B * N // CHUNK

    def sb(name, shape, dt=F32):
        return ctx.enter_context(nc.sbuf_tensor(name, shape, dt))

    with ExitStack() as norm:
        ps_centred = norm.enter_context(nc.psum_tensor("ps_centred", [128, 2, CHUNK], F32))
        ps_var = norm.enter_context(nc.psum_tensor("ps_var2", [128, 2, CHUNK], F32))
        squares, log_var, rstd = (norm.enter_context(nc.sbuf_tensor(n, [C, 2, CHUNK], F32))
                                  for n in ("squares2", "log_var2", "rstd2"))
        eps = norm.enter_context(nc.sbuf_tensor("eps2", [C, 1], F32))
        eps_set = sem("eps_set")
        s = {n: sem(n + "_2") for n in ("centred_ready", "squares_ready", "var_ready", "log_ready",
                                        "rstd_ready", "normed_ready")}
        with nc.Block() as block:
            @block.gpsimd
            def _(pool):
                nc.gpsimd.memset(eps[:, :], EPS).then_inc(eps_set, 1)

            @block.tensor
            def _(pe):
                def centre(k, par):
                    need(pe, s["normed_ready"], k - 1)
                    nc.tensor.matmul(ps_centred[0:C, par, :], center[:, :], stream[:, bass.ds(k * CHUNK, CHUNK)],
                                     start=True, stop=True).then_inc(s["centred_ready"], 1)

                def spread(k, par):
                    pe.wait_ge(s["squares_ready"], k + 1)
                    need(pe, s["log_ready"], k - 1)
                    nc.tensor.matmul(ps_var[0:C, par, :], average[:, :], squares[:, par, :],
                                     start=True, stop=True).then_inc(s["var_ready"], 1)

                def step(k, half, par):
                    if not is_image(k, CHUNKS - 1):
                        centre(k + 1, 1 - par)
                    spread(k, par)

                centre(0, 0)
                chunk_loop(pe, step)

            @block.scalar
            def _(act):
                act.wait_ge(eps_set, 1)

                def square(k, par):
                    act.wait_ge(s["centred_ready"], k + 1)
                    need(act, s["var_ready"], k - 1)
                    nc.scalar.activation(squares[:, par, :], ps_centred[0:C, par, :],
                                         ACT.Square).then_inc(s["squares_ready"], 1)

                def step(k, half, par):
                    if not is_image(k, CHUNKS - 1):
                        square(k + 1, 1 - par)
                    act.wait_ge(s["var_ready"], k + 1)
                    need(act, s["rstd_ready"], k - 1)
                    nc.scalar.activation(log_var[:, par, :], ps_var[0:C, par, :], ACT.Ln,
                                         bias=eps[:, 0:1]).then_inc(s["log_ready"], 1)
                    act.wait_ge(s["log_ready"], k + 1)
                    need(act, s["normed_ready"], k - 1)
                    nc.scalar.activation(rstd[:, par, :], log_var[:, par, :], ACT.Exp,
                                         scale=-0.5).then_inc(s["rstd_ready"], 1)

                nc.scalar.preload_act_table_set("natural_log_exp_and_others")
                square(0, 0)
                chunk_loop(act, step)

            @block.vector
            def _(dve):
                def step(k, half, par):
                    dve.wait_ge(s["rstd_ready"], k + 1)
                    nc.vector.tensor_tensor(mixed[:, bass.ds(k * CHUNK, CHUNK)], ps_centred[0:C, par, :],
                                            rstd[:, par, :], ALU.mult).then_inc(s["normed_ready"], 1)

                chunk_loop(dve, step)

    fc1 = sb("fc1_scaled", [C, HID])
    fc1_b = sb("fc1_b_folded", [128, HT])
    summed = sb("summed", [C, 2, CHUNK])
    hidden = sb("hidden", [128, 2, HT, CHUNK])
    ps_hidden = ctx.enter_context(nc.psum_tensor("ps_hidden", [128, 2 * HT, CHUNK], F32))
    ps_y = ctx.enter_context(nc.psum_tensor("ps_y", [128, 2, CHUNK], F32))
    set_up = sem("set_up_mlp")
    pe_set = sem("pe_set_mlp")
    s = {n: sem(n) for n in ("hidden_ready", "gelu_ready", "y_ready", "sum_ready", "mixed_ready", "stats_ready")}
    QUARTERS = 4
    block = ctx.enter_context(nc.Block())

    @block.tensor
    def _(pe):
        for k in range(HT):
            nc.tensor.matmul(ps_y[:, 0, k:k + 1], w["fc1"][:, k * 128:(k + 1) * 128], w["norm2_b"][:, :],
                             start=True, stop=True, skip_group_check=True).then_inc(pe_set, 1)
        pe.wait_ge(set_up, 2)

        def up(k, par):
            need(pe, s["gelu_ready"], (k - 1) * HT)
            for h in range(HT):
                nc.tensor.matmul(ps_hidden[:, par * HT + h, :], fc1[:, h * 128:(h + 1) * 128],
                                 mixed[:, bass.ds(k * CHUNK, CHUNK)], start=True, stop=True).then_inc(s["hidden_ready"], 1)

        def down(k, par):
            need(pe, s["sum_ready"], k - 1)
            for h in range(HT):
                pe.wait_ge(s["gelu_ready"], k * HT + h + 1)
                mm = nc.tensor.matmul(ps_y[0:C, par, :], w["fc2"][:, h, :], hidden[:, par, h, :],
                                      start=(h == 0), stop=(h == HT - 1))
            mm.then_inc(s["y_ready"], 1)

        def step(k, half, par):
            if not is_image(k, CHUNKS - 1):
                up(k + 1, 1 - par)
            down(k, par)

        up(0, 0)
        chunk_loop(pe, step)

    @block.scalar
    def _(act):
        act.wait_ge(set_up, 2)

        def step(k, half, par):
            need(act, s["y_ready"], k - 1)
            for h in range(HT):
                act.wait_ge(s["hidden_ready"], k * HT + h + 1)
                nc.scalar.activation(hidden[:, par, h, :], ps_hidden[:, par * HT + h, :], ACT.Gelu,
                                     bias=fc1_b[:, h:h + 1]).then_inc(s["gelu_ready"], 1)

        chunk_loop(act, step)

    @block.vector
    def _(dve):
        nc.vector.tensor_scalar(fc1[:, :], w["fc1"][:, :], w["norm2_g"][:, 0:1], None, ALU.mult).then_inc(set_up, 1)
        dve.wait_ge(pe_set, HT)
        nc.vector.tensor_tensor(fc1_b[:, :], ps_y[:, 0, 0:HT], w["fc1_b"][:, :], ALU.add).then_inc(set_up, 1)

        def step(k, half, par):
            dve.wait_ge(s["y_ready"], k + 1)
            need(dve, s["mixed_ready"], (k - 1) * 2 * QUARTERS)
            nc.vector.scalar_tensor_tensor(out=summed[:, par, :], in0=ps_y[0:C, par, :], scalar=w["fc2_b"][:, 0:1],
                                           in1=stream[:, bass.ds(k * CHUNK, CHUNK)],
                                           op0=ALU.add, op1=ALU.add).then_inc(s["sum_ready"], 1)
            dve.wait_ge(s["sum_ready"], k + 1)
            for j in range(2):
                src = windows(summed[:, par, j * N:(j + 1) * N])
                dst = mixed[:, bass.ds(k * CHUNK + j * N, N)].rearrange("p (a r b c) -> p a r b c", a=4, r=SS, b=4)
                blocks, order = (slice(1, 4, 2), slice(0, 3, 2)), (slice(None), slice(None, None, -1))
                for top in range(2):
                    for left in range(2):
                        rows, cs = slice(top * SS, top * SS + SS), slice(left * SS, left * SS + SS)
                        nc.vector.tensor_copy(
                            dst[:, blocks[top], :, blocks[left], :].rearrange("p a r b c -> p a b r c"),
                            src[:, order[top], order[left], rows, cs]).then_inc(s["mixed_ready"], 1)
            for j in range(2):
                dve.wait_ge(s["mixed_ready"], k * 2 * QUARTERS + (j + 1) * QUARTERS)
                nc.vector.bn_stats(stats[:, bass.ds(k * 2 + j, 1), :], mixed[:, bass.ds(k * CHUNK + j * N, N)]).then_inc(s["stats_ready"], 1)

        chunk_loop(dve, step)


def channel_attention(nc, ctx, sem, mixed, stats, ident, average, w, stack_ones, out):
    def sb(name, shape, dt=F32):
        return ctx.enter_context(nc.sbuf_tensor(name, shape, dt))

    def bank(name, count=1):
        return ctx.enter_context(nc.psum_tensor(name, [128, count, 512], F32))

    moments = sb("moments", [C, B, 2])
    mean2 = sb("mean2", [C, B, 2])
    mean = sb("mean", [C, B])
    spread2 = sb("spread2", [C, B, 2])
    log_var = sb("log_var3", [C, B])
    eps = sb("eps3", [C, 1])
    products = sb("products", [3 * SET, SETS, SIDE, STACK])
    conv_w = sb("conv_w", [STACK, SETS, SIDE, 3 * SET])
    final_w = sb("final_w", [C, C])
    recip_alpha = sb("recip_alpha", [C, 1])
    moment = sb("moment", [C, 2])
    x_scaled = sb("x_scaled", [C, N])
    x_gained = sb("x_gained", [C, N])
    x_pad = sb("x_pad", [SETS * SET, 2, PADW, PADW])
    x_stack = sb("x_stack", [STACK, 2, SETS, ROWS])
    qkv = sb("qkv", [3 * SET, 2, SETS, N])
    v_sb = sb("v_sb", [C, 2, N])
    tokens = sb("tokens", [128, 2, 2, SETS * SET])
    logits = sb("logits", [C, C])
    peak = sb("peak3", [C, 1])
    neg_peak = sb("neg_peak", [C, 1])
    row_sum = sb("row_sum", [C, 1])
    recip_sum = sb("recip_sum", [C, 1])
    attn = sb("attn", [C, C])
    av_sb = sb("av_sb", [C, N])
    y_sb = sb("y_sb", [C, 2, N])
    padded_x = nc.dram_tensor("padded_x", (B, SETS * SET, PADW * PADW), F32, kind="Internal").ap()

    ps_qkv = bank("ps_qkv", SETS)
    ps_tok_bank = bank("ps_tok")
    ps_tok = ps_tok_bank[:, 0, 0:2 * SETS * 2 * SET].rearrange("p (n s c) -> p n s c", n=2, s=SETS)
    ps_gram = bank("ps_gram")[0:C, 0, 0:C]
    ps_av = bank("ps_av")[0:C, 0, 0:N]
    ps_y_bank = bank("ps_y3")
    ps_y = ps_y_bank[0:C, 0, 0:N]
    ps_moments = ps_y_bank[0:C, 0, 0:2 * B]

    zeroed = sem("zeroed3")
    ones_in = sem("ones_in")
    moments_set = sem("moments_set")
    moments_pe = sem("moments_pe")
    log_set = sem("log_set")
    rstd_set = sem("rstd_set")
    products_set = sem("products_set")
    weights_turned = sem("weights_turned")
    weights_copied = sem("weights_copied")
    alpha_set = sem("alpha_set")
    written = [sem("written0"), sem("written1")]
    stacked = [sem("stacked0"), sem("stacked1")]
    v_moved = [sem("v_moved0"), sem("v_moved1")]
    out_done = [sem("out_done0"), sem("out_done1")]
    s = {n: sem(n + "_3") for n in (
        "moment_ready", "scaled", "gained", "normed", "x_padded", "conv_ready", "evacuated", "tok_ready",
        "tok_copied", "gram_ready", "logits_ready", "peak_ready", "neg_ready", "exp_ready", "recip_ready",
        "attn_ready", "av_ready", "av_copied", "final_ready", "y_ready")}
    SHIFT_LOADS, MOVES = SIDE, SETS

    def pads_zeroed(engine):
        engine.wait_ge(zeroed, 3)

    block = ctx.enter_context(nc.Block())

    @block.sync
    def _(sp):
        sp.dma_start(x_stack[SIDE * SET:STACK, :, :, :], stack_ones).then_inc(ones_in, 16)
        pads_zeroed(sp)

        def write(t, par):
            pads_zeroed(sp)
            sp.wait_ge(s["x_padded"], t + 1)
            sp.dma_start(padded_x[bass.ds(t, 1)].rearrange("a p m -> (a p) m"), x_pad[:, par, :, :].rearrange("p r c -> p (r c)")).then_inc(written[par], 16)

        def stack(t, half, par):
            pads_zeroed(sp)
            sp.wait_ge(written[par], (half + 1) * 16)
            need(sp, s["conv_ready"], (t - 1) * SETS)
            for i in range(SIDE):
                sp.dma_start(x_stack[i * SET:(i + 1) * SET, par, :, :],
                             padded_x[bass.ds(t, 1), :, i * PADW:i * PADW + ROWS].rearrange("a (s c) m -> (a c) s m", c=SET)
                             ).then_inc(stacked[par], 16)

        def store(t, par):
            pads_zeroed(sp)
            sp.wait_ge(s["y_ready"], t + 1)
            sp.dma_start(out[bass.ds(t, 1)].rearrange("a c h w -> c (a h w)"), y_sb[:, par, :]).then_inc(out_done[par], 16)

        write(0, 0)
        stack(0, 0, 0)
        write(1, 1)
        stack(1, 0, 1)
        write(2, 0)

        def step(t, half, par):
            if not past(t + 2):
                stack(t + 2, half + 1, par)
            if not past(t + 3):
                write(t + 3, 1 - par)
            if not is_image(t, 0):
                store(t - 1, 1 - par)

        image_loop(sp, step, tail=2)
        store(B - 1, 1)
        for par in range(2):
            sp.wait_ge(out_done[par], 16 * (B // 2))

    @block.gpsimd
    def _(pool):
        nc.gpsimd.memset(products[:, :, :, :], 0.0).then_inc(zeroed, 1)
        nc.gpsimd.memset(eps[:, :], EPS).then_inc(zeroed, 1)
        nc.gpsimd.memset(x_pad[:, :, :, :], 0.0).then_inc(zeroed, 1)

    @block.scalar
    def _(act):
        nc.scalar.preload_act_table_set("natural_log_exp_and_others")
        pads_zeroed(act)
        act.wait_ge(moments_set, 7)
        nc.scalar.activation(log_var[:, :], spread2[:, :, 0], ACT.Ln, scale=0.5, bias=eps[:, 0:1]).then_inc(log_set, 1)
        act.wait_ge(log_set, 1)
        nc.scalar.activation(moments[:, :, 0], log_var[:, :], ACT.Exp, scale=-0.5).then_inc(rstd_set, 1)
        act.wait_ge(moments_set, 8)

        def scale(t):
            pads_zeroed(act)
            need(act, s["scaled"], t)
            nc.scalar.copy(moment[:, :], moments[:, bass.ds(t, 1), :].rearrange("p a b -> p (a b)")).then_inc(s["moment_ready"], 1)
            pads_zeroed(act)
            act.wait_ge(s["moment_ready"], t + 1)
            need(act, s["gained"], t)
            nc.scalar.activation(x_scaled[:, :], mixed[:, bass.ds(t * N, N)], ACT.Identity, bias=moment[:, 1:2],
                                 scale=moment[:, 0:1]).then_inc(s["scaled"], 1)

        def pad_x(t, par):
            pads_zeroed(act)
            act.wait_ge(s["normed"], t + 1)
            nc.scalar.copy(x_pad[0:C, par, 1:H + 1, 1:W + 1], grid(mixed[:, bass.ds(t * N, N)])).then_inc(s["x_padded"], 1)

        def evacuate(t, half, par, g):
            act.wait_ge(s["conv_ready"], t * SETS + g + 1)
            need(act, s["tok_ready"], t - 1)
            need(act, v_moved[par], half * 16 * MOVES)
            nc.scalar.copy(qkv[:, par, g, :], ps_qkv[0:3 * SET, g, 0:N]).then_inc(s["evacuated"], 1)

        def move_v(t, par):
            act.wait_ge(s["evacuated"], (t + 1) * SETS)
            need(act, s["av_ready"], t - 1)
            for g in range(SETS):
                count = min(SET, C - g * SET)
                act.dma_start(v_sb[g * SET:g * SET + count, par, :],
                              qkv[2 * SET:2 * SET + count, par, g, :]).then_inc(v_moved[par], 16)

        def exponent(t):
            act.wait_ge(s["neg_ready"], t + 1)
            need(act, s["recip_ready"], t)
            nc.scalar.activation(logits[:, :], logits[:, :], ACT.Exp, bias=neg_peak[:, 0:1],
                                 accum_out=row_sum[:, 0:1]).then_inc(s["exp_ready"], 1)

        def copy_av(t):
            act.wait_ge(s["av_ready"], t + 1)
            need(act, s["final_ready"], t)
            nc.scalar.copy(av_sb[:, :], ps_av).then_inc(s["av_copied"], 1)

        scale(0)
        pad_x(0, 0)
        scale(1)
        pad_x(1, 1)
        for g in range(SETS):
            act.wait_ge(weights_turned, SIDE * (g + 1))
            nc.scalar.copy(conv_w[:, g, :, :], ps_qkv[0:STACK, g, 0:SIDE * 3 * SET].rearrange("p (j m) -> p j m", j=SIDE)).then_inc(weights_copied, 1)
        act.wait_ge(weights_turned, SIDE * SETS + 1)
        nc.scalar.copy(final_w[:, :], ps_gram).then_inc(weights_copied, 1)
        scale(2)
        pad_x(2, 0)
        scale(3)
        for g in range(SETS):
            evacuate(0, 0, 0, g)

        def step(t, half, par):
            if not is_image(t, 0):
                copy_av(t - 1)
            move_v(t, par)
            if not past(t + 3):
                pad_x(t + 3, 1 - par)
            if not past(t + 1):
                evacuate(t + 1, half + par, 1 - par, 0)
            if not past(t + 4):
                scale(t + 4)
            exponent(t)
            if not past(t + 1):
                evacuate(t + 1, half + par, 1 - par, 1)
                evacuate(t + 1, half + par, 1 - par, 2)

        image_loop(act, step, tail=2)
        copy_av(B - 1)

    @block.vector
    def _(dve):
        means, deviations = stats[:, :, 1::3], stats[:, :, 2::3]
        dve.wait_ge(moments_pe, 1)
        nc.vector.tensor_copy(mean2[:, :, :], ps_moments.rearrange("p (t e) -> p t e", e=2)).then_inc(moments_set, 1)
        dve.wait_ge(moments_set, 1)
        nc.vector.tensor_tensor(mean[:, :], mean2[:, :, 0], mean2[:, :, 1], ALU.add).then_inc(moments_set, 1)
        dve.wait_ge(moments_set, 2)
        nc.vector.tensor_scalar(mean[:, :], mean[:, :], 0.5, None, ALU.mult).then_inc(moments_set, 1)
        dve.wait_ge(moments_set, 3)
        nc.vector.tensor_tensor(mean2[:, :, :], means, mean[:, :].unsqueeze(2).to_broadcast((C, B, 2)),
                                ALU.subtract).then_inc(moments_set, 1)
        dve.wait_ge(moments_set, 4)
        nc.vector.tensor_tensor(spread2[:, :, :], mean2[:, :, :], mean2[:, :, :], ALU.mult).then_inc(moments_set, 1)
        dve.wait_ge(moments_set, 5)
        nc.vector.scalar_tensor_tensor(out=spread2[:, :, :], in0=deviations, scalar=2.0 / N, in1=spread2[:, :, :],
                                       op0=ALU.mult, op1=ALU.add).then_inc(moments_set, 1)
        dve.wait_ge(moments_pe, 2)
        nc.vector.tensor_reduce(spread2[:, :, 0], ps_moments.rearrange("p (t e) -> p t e", e=2), AX_X,
                                ALU.add).then_inc(moments_set, 1)
        dve.wait_ge(rstd_set, 1)
        nc.vector.scalar_tensor_tensor(out=moments[:, :, 1], in0=mean[:, :], scalar=-1.0, in1=moments[:, :, 0],
                                       op0=ALU.mult, op1=ALU.mult).then_inc(moments_set, 1)

        def affine(t, half, par):
            dve.wait_ge(s["scaled"], t + 1)
            need(dve, s["normed"], t)
            nc.vector.tensor_tensor(x_gained[:, :], x_scaled[:, :], w["ln_g"][:, :], ALU.mult).then_inc(s["gained"], 1)
            dve.wait_ge(s["gained"], t + 1)
            need(dve, written[par], half * 16)
            nc.vector.tensor_tensor(mixed[:, bass.ds(t * N, N)], x_gained[:, :], w["ln_b"][:, :],
                                    ALU.add).then_inc(s["normed"], 1)

        def copy_tokens(t):
            dve.wait_ge(s["tok_ready"], t + 1)
            need(dve, s["gram_ready"], t)
            for n in range(2):
                nc.vector.tensor_copy(tokens[:, n, :, :].rearrange("p k (s c) -> p s k c", s=SETS),
                                      ps_tok[:, n, :, :].rearrange("p s (k c) -> p s k c", k=2)).then_inc(s["tok_copied"], 1)

        def make_logits(t):
            dve.wait_ge(s["gram_ready"], t + 1)
            need(dve, s["attn_ready"], t)
            nc.vector.scalar_tensor_tensor(out=logits[:, :], in0=ps_gram, scalar=recip_alpha[:, 0:1],
                                           in1=w["block_mask"][:, :], op0=ALU.mult, op1=ALU.add).then_inc(s["logits_ready"], 1)
            dve.wait_ge(s["logits_ready"], t + 1)
            need(dve, s["neg_ready"], t)
            nc.vector.tensor_reduce(peak[:, :], logits[:, :], AX_X, ALU.max).then_inc(s["peak_ready"], 1)
            dve.wait_ge(s["peak_ready"], t + 1)
            need(dve, s["exp_ready"], t)
            nc.vector.tensor_scalar(neg_peak[:, :], peak[:, :], -1.0, None, ALU.mult).then_inc(s["neg_ready"], 1)

        def normalise(t):
            dve.wait_ge(s["exp_ready"], t + 1)
            nc.vector.reciprocal(recip_sum[:, :], row_sum[:, :]).then_inc(s["recip_ready"], 1)
            dve.wait_ge(s["recip_ready"], t + 1)
            need(dve, s["av_ready"], t)
            nc.vector.tensor_scalar(attn[:, :], logits[:, :], recip_sum[:, 0:1], None, ALU.mult).then_inc(s["attn_ready"], 1)

        def finish(t, half, par):
            dve.wait_ge(s["final_ready"], t + 1)
            need(dve, out_done[par], half * 16)
            nc.vector.scalar_tensor_tensor(out=y_sb[:, par, :], in0=ps_y, scalar=w["final_b"][:, 0:1],
                                           in1=mixed[:, bass.ds(t * N, N)], op0=ALU.add, op1=ALU.add).then_inc(s["y_ready"], 1)

        affine(0, 0, 0)
        dve.wait_ge(zeroed, 3)
        for g in range(SETS):
            taps = w["taps"][:, g, :].rearrange("p (i j) -> p j i", i=SIDE)
            nc.vector.tensor_tensor(products[:, g, :, 0:SIDE * SET].rearrange("p j (i c) -> p j i c", i=SIDE),
                                    w["point"][:, g, :].unsqueeze(1).unsqueeze(1).to_broadcast((3 * SET, SIDE, SIDE, SET)),
                                    taps.unsqueeze(3).to_broadcast((3 * SET, SIDE, SIDE, SET)),
                                    ALU.mult).then_inc(products_set, 1)
            nc.vector.tensor_scalar(products[:, g, :, SIDE * SET:SIDE * SET + SIDE], taps, w["point_b"][:, g:g + 1], None,
                                    ALU.mult).then_inc(products_set, 1)
            nc.vector.tensor_copy(products[:, g, 0, STACK - 1:STACK], w["taps_b"][:, g:g + 1]).then_inc(products_set, 1)
        affine(1, 0, 1)
        nc.vector.reciprocal(recip_alpha[:, :], w["alpha"][:, :]).then_inc(alpha_set, 1)
        affine(2, 1, 0)
        dve.wait_ge(alpha_set, 1)

        def step(t, half, par):
            if not past(t + 3):
                affine(t + 3, half + 1 + par, 1 - par)
            copy_tokens(t)
            if not is_image(t, 0):
                finish(t - 1, half if par else half - 1, 1 - par)
            make_logits(t)
            normalise(t)

        image_loop(dve, step, tail=2)
        finish(B - 1, B // 2 - 1, 1)

    @block.tensor
    def _(pe):
        nc.tensor.matmul(ps_moments, average[:, :], stats[:, :, 1::3], start=True, stop=True).then_inc(moments_pe, 1)
        pe.wait_ge(moments_set, 6)
        nc.tensor.matmul(ps_moments, average[:, :], spread2[:, :, :], start=True, stop=True).then_inc(moments_pe, 1)
        for g in range(SETS):
            pe.wait_ge(products_set, 3 * (g + 1))
            for j in range(SIDE):
                nc.tensor.transpose(ps_qkv[0:STACK, g, j * 3 * SET:(j + 1) * 3 * SET], products[:, g, j, :],
                                    ident[0:3 * SET, 0:3 * SET]).then_inc(weights_turned, 1)
        nc.tensor.transpose(ps_gram, w["final"][:, :], ident[0:C, 0:C]).then_inc(weights_turned, 1)
        pe.wait_ge(weights_copied, SETS + 1)
        pe.wait_ge(ones_in, 16)

        def convolve(t, half, par, g):
            pe.wait_ge(stacked[par], (half + 1) * 16 * SHIFT_LOADS)
            need(pe, s["evacuated"], (t - 1) * SETS + g + 1)
            for j in range(SIDE):
                mm = nc.tensor.matmul(ps_qkv[0:3 * SET, g, 0:N], conv_w[:, g, j, :],
                                      grid(x_stack[:, par, g, :], PADW)[:, :, j:j + W],
                                      start=(j == 0), stop=(j == SIDE - 1))
            mm.then_inc(s["conv_ready"], 1)

        def turn_tokens(t, par):
            need(pe, s["tok_copied"], t * 2)
            for g in range(SETS):
                pe.wait_ge(s["evacuated"], t * SETS + g + 1)
                for n in range(2):
                    mm = nc.tensor.transpose(ps_tok[:, n, g, :], qkv[0:2 * SET, par, g, n * 128:(n + 1) * 128],
                                             ident[0:2 * SET, 0:2 * SET])
            mm.then_inc(s["tok_ready"], 1)

        def gram(t):
            pe.wait_ge(s["tok_copied"], (t + 1) * 2)
            need(pe, s["logits_ready"], t)
            for n in range(2):
                mm = nc.tensor.matmul(ps_gram, tokens[:, n, 1, 0:C], tokens[:, n, 0, 0:C], start=(n == 0), stop=(n == 1))
            mm.then_inc(s["gram_ready"], 1)

        def attend(t, half, par):
            pe.wait_ge(s["attn_ready"], t + 1)
            pe.wait_ge(v_moved[par], (half + 1) * 16 * MOVES)
            need(pe, s["av_copied"], t)
            nc.tensor.matmul(ps_av, attn[:, :], v_sb[:, par, :], start=True, stop=True).then_inc(s["av_ready"], 1)

        def finalise(t):
            pe.wait_ge(s["av_copied"], t + 1)
            need(pe, s["y_ready"], t)
            nc.tensor.matmul(ps_y, final_w[:, :], av_sb[:, :], start=True, stop=True).then_inc(s["final_ready"], 1)

        for g in range(SETS):
            convolve(0, 0, 0, g)

        def step(t, half, par):
            turn_tokens(t, par)
            if not past(t + 1):
                convolve(t + 1, half + par, 1 - par, 0)
            if not is_image(t, 0):
                finalise(t - 1)
            gram(t)
            if not past(t + 1):
                convolve(t + 1, half + par, 1 - par, 1)
                convolve(t + 1, half + par, 1 - par, 2)
            attend(t, half, par)

        image_loop(pe, step, tail=2)
        finalise(B - 1)


_INS = ['x', 'L0_conv_qkv_w', 'L0_conv_qkv_b', 'L0_conv_proj_w', 'L0_conv_proj_b', 'L0_conv_rel_bias',
        'L0_conv_norm1_g', 'L0_conv_norm1_b', 'L0_conv_norm2_g', 'L0_conv_norm2_b', 'L0_conv_fc1_w',
        'L0_conv_fc1_b', 'L0_conv_fc2_w', 'L0_conv_fc2_b', 'L1_conv_ln_g', 'L1_conv_ln_b', 'L1_conv_wq_p',
        'L1_conv_bq_p', 'L1_conv_wq_d', 'L1_conv_bq_d', 'L1_conv_wk_p', 'L1_conv_bk_p', 'L1_conv_wk_d',
        'L1_conv_bk_d', 'L1_conv_wv_p', 'L1_conv_bv_p', 'L1_conv_wv_d', 'L1_conv_bv_d', 'L1_conv_alpha',
        'L1_conv_w_f', 'L1_conv_b_f']


def constants():
    f = np.float32
    head_mask = np.zeros((C, GROUP), f)
    for c in range(C):
        head_mask[c, (c // HD) % GROUP] = 1
    region = np.repeat([0, 1, 2], [H - WS, WS - SS, SS])
    label = region[:, None] * 3 + region[None, :]
    shift = np.zeros((2, WN, PAIRS, WN), f)
    for p in range(PAIRS):
        for w in range(2):
            win = label[p * WS:(p + 1) * WS, w * WS:(w + 1) * WS].reshape(-1)
            shift[w, :, p, :] = np.where(win[:, None] != win[None, :], -10.0, 0.0)
    head = np.arange(C) // HC
    ones = np.pad(np.ones((H, W), f), 1).reshape(-1)
    stack = np.stack([ones[i * PADW:i * PADW + ROWS] for i in range(SIDE)] + [np.ones(ROWS, f)])
    return {
        "c_stack_ones": np.ascontiguousarray(np.broadcast_to(stack[:, None, None], (SIDE + 1, 2, SETS, ROWS))),
        "c_ident": np.eye(128, dtype=f),
        "c_center": (np.eye(C) - 1.0 / C).astype(f),
        "c_average": np.full((C, C), 1.0 / C, f),
        "c_head_mask": head_mask,
        "c_shift_mask": shift.reshape(128, PAIRS, WN),
        "c_block_mask": np.where(head[:, None] == head[None, :], 0.0, BLOCKED).astype(f),
    }


def kernel(**inputs):
    import concourse.bacc as _bacc
    from concourse.bass_utils import run_bass_kernel_spmd as _run

    nc = _bacc.Bacc("TRN2", target_bir_lowering=False, num_devices=1)
    arrays, args = {}, {}
    given = {name: np.ascontiguousarray(inputs[name]) for name in _INS}
    for name, v in {**given, **constants()}.items():
        arrays[f"in_{name}"] = v
        args[name] = nc.dram_tensor(f"in_{name}", v.shape, mybir.dt.from_np(v.dtype), kind="ExternalInput").ap()
    args["out"] = nc.dram_tensor("out_0", (B, C, H, W), F32, kind="ExternalOutput").ap()
    build(nc, args)
    r = _run(nc, [arrays], core_ids=[0])
    return r.results[0]["out_0"]
```

```python
from contextlib import ExitStack

import numpy as np

import concourse.bass as bass
from concourse import mybir

ALU = mybir.AluOpType
ACT = mybir.ActivationFunctionType
AX_X = mybir.AxisListType.X
F32 = mybir.dt.float32

B, C, H, W = 32, 96, 16, 16
N = H * W
HEADS, HD = 12, 8
WS, SS = 8, 4
WN = WS * WS
GROUP = 4
NG = HEADS // GROUP
PAIRS = 2
HP = HEADS // 2
BANK_HP = 512 // 128
SC = HEADS * WN
VC = HD + 1
HID = 4 * C
HT = HID // 128
REL = 2 * WS - 1
NH2, HC = 8, 12
SET_HEADS = 3
SET = SET_HEADS * HC
SETS = -(-NH2 // SET_HEADS)
EPS = 1e-5
SCALE = HD ** -0.5
PADW = W + 2
SIDE = 3
TAPS = SIDE * SIDE
STACK = SIDE * SET + SIDE + 1
ROWS = H * PADW
CHUNK = 2 * N
BLOCKED = -1e30


def need(engine, semaphore, count):
    if isinstance(count, int) and count <= 0:
        return
    engine.wait_ge(semaphore, count)


def led_image_loop(engine, step, tail=1, between=None):
    step(-2, -1, 0)
    if between:
        between()
    step(-1, -1, 1)
    image_loop(engine, step, tail)


def image_loop(engine, step, tail=1, lead=1, between=None, start=0):
    for half in range(lead):
        for par in range(2):
            if half * 2 + par >= start:
                step(half * 2 + par, half, par)
        if between:
            between(half)
    with engine.Fori(lead, B // 2 - tail) as i:
        step(i * 2, i, 0)
        step(i * 2 + 1, i, 1)
    for half in range(B // 2 - tail, B // 2):
        step(half * 2, half, 0)
        step(half * 2 + 1, half, 1)


def real(t):
    return not isinstance(t, int) or 0 <= t < B


def up_to(t):
    return min(t + 1, B) if isinstance(t, int) else t + 1


def past(t):
    return isinstance(t, int) and t >= B


def is_image(t, other):
    return isinstance(t, int) and t == other


def build(nc, a):
    ctx = ExitStack()
    with ctx:
        def sb(name, shape, dt=F32):
            return ctx.enter_context(nc.sbuf_tensor(name, shape, dt))

        def sem(name):
            return ctx.enter_context(nc.semaphore(name))

        stream = sb("stream", [C, B * N])
        ident = sb("ident", [128, 128])
        center = sb("center", [C, C])
        average = sb("average", [C, C])
        w = {name: sb(name, shape) for name, shape in (
            ("fc1", [C, HID]), ("fc2", [128, HT, C]), ("fc1_b", [128, HT]), ("fc2_b", [C, 1]),
            ("norm2_g", [C, 1]), ("norm2_b", [C, 1]),
            ("ln_g", [C, N]), ("ln_b", [C, N]),
            ("point", [3 * SET, SETS, SET]), ("point_b", [3 * SET, SETS]),
            ("taps", [3 * SET, SETS, TAPS]), ("taps_b", [3 * SET, SETS]),
            ("final", [C, C]), ("final_b", [C, 1]), ("alpha", [C, 1]),
            ("block_mask", [C, C]))}
        weights_in = sem("weights_in")
        zeroed_points = sem("zeroed_points")
        with ExitStack() as p1:
            window_attention(nc, p1, a, sem, stream, ident, center, average, w, weights_in, zeroed_points)
        mixed = sb("mixed", [C, B * N])
        stats = sb("stats", [C, B, 6])
        with ExitStack() as p2:
            mlp(nc, p2, sem, stream, mixed, stats, center, average, w)
        with ExitStack() as p3:
            channel_attention(nc, p3, sem, stream, mixed, stats, ident, average, w, a["c_stack_ones"], a["out"])


def grid(ap, width=W):
    return ap.rearrange("p (r c) -> p r c", c=width)


def windows(ap):
    return ap.rearrange("p (a w r c) -> p a w r c", a=2, w=2, r=WS)


def weight_loads(a, w):
    def column(name, k=0, n=C):
        return a[name][k * n:(k + 1) * n].rearrange("(c a) -> c a", a=1)

    loads = [
        (w["fc1"][:, :], a["L0_conv_fc1_w"]),
        (w["fc2"][:, :, :], a["L0_conv_fc2_w"].rearrange("(k p) c -> p k c", p=128)),
        (w["fc2_b"][:, :], column("L0_conv_fc2_b")),
        (w["norm2_g"][:, :], column("L0_conv_norm2_g")),
        (w["norm2_b"][:, :], column("L0_conv_norm2_b")),
        (w["ln_g"][:, :], a["L1_conv_ln_g"].rearrange("c h w -> c (h w)")),
        (w["ln_b"][:, :], a["L1_conv_ln_b"].rearrange("c h w -> c (h w)")),
        (w["final"][:, :], a["L1_conv_w_f"]),
        (w["final_b"][:, :], column("L1_conv_b_f")),
        (w["block_mask"][:, :], a["c_block_mask"]),
    ]
    loads += [(w["fc1_b"][:, k:k + 1], column("L0_conv_fc1_b", k, 128)) for k in range(HT)]
    for k, n in enumerate("qkv"):
        for j in range(SET_HEADS):
            at = slice(j * HC, (j + 1) * HC)
            heads = a[f"L1_conv_w{n}_p"][j::SET_HEADS]
            loads.append((w["point"][k * SET + j * HC:k * SET + (j + 1) * HC, 0:heads.shape[0], at],
                          heads.rearrange("s o c -> o s c")))
        for name, flat in (("point_b", a[f"L1_conv_b{n}_p"].rearrange("h (c a) -> (h c) a", a=1)),
                           ("taps", a[f"L1_conv_w{n}_d"].rearrange("c a i j -> c (a i j)")),
                           ("taps_b", a[f"L1_conv_b{n}_d"].rearrange("(c a) -> c a", a=1))):
            for g in range(SETS):
                count = min(SET, C - g * SET)
                loads.append((w[name][k * SET:k * SET + count, g] if name == "taps" else
                              w[name][k * SET:k * SET + count, g:g + 1], flat[g * SET:g * SET + count]))
    loads += [(w["alpha"][h * HC:(h + 1) * HC, :],
               a["L1_conv_alpha"][h:h + 1].rearrange("(b a) -> b a", a=1).to_broadcast((HC, 1))) for h in range(NH2)]
    return loads


def window_attention(nc, ctx, a, sem, stream, ident, center, average, w_late, weights_in, zeroed_points):
    def sb(name, shape, dt=F32):
        return ctx.enter_context(nc.sbuf_tensor(name, shape, dt))

    def bank(name, count=1):
        return ctx.enter_context(nc.psum_tensor(name, [128, count, 512], F32))

    head_mask = sb("head_mask", [C, GROUP])
    shift_mask = sb("shift_mask", [128, PAIRS, WN])
    rel_rows = sb("rel_rows", [128, WN, HEADS])
    bias = sb("bias", [128, PAIRS, SC])
    w_in = sb("w_in", [C, 3 * C])
    w_qkv = sb("w_qkv", [C, 3 * C])
    w_proj = sb("w_proj", [C, C])
    cols = sb("cols", [C, 6])
    b_q = sb("b_q", [C, 1])
    b_k = sb("b_k", [C, 1])
    b_v = sb("b_v", [C, 1])
    b_proj = sb("b_proj", [C, 1])
    x_in = sb("x_in", [C, 2, N])
    squares = sb("squares", [C, N])
    log_var = sb("log_var", [C, N])
    eps = sb("eps", [C, 1])
    rstd = sb("rstd", [C, N])
    normed = sb("normed", [C, N])
    q_sb = sb("q_sb", [C, N])
    k_blocks = sb("k_blocks", [C, GROUP, N])
    v_blocks = sb("v_blocks", [128, 2, PAIRS, HP + 2, 2, 2, VC])
    scores = sb("scores", [128, PAIRS, SC])
    peak = sb("peak", [128, PAIRS, HEADS])
    probs_t = sb("probs_t", [128, SC])
    recip = sb("recip", [128, HEADS])
    heads_out = sb("heads_out", [128, C])
    out_t = sb("out_t", [C, 2, N])

    ps_scores = bank("ps_scores", NG)
    ps_probs = bank("ps_probs", 2)
    ps_out = bank("ps_out")
    ps_a = bank("ps_a")
    ps_b = bank("ps_b")
    centred = ps_a[0:C, 0, 0:N]
    ps_var = ps_a[0:C, 0, N:2 * N]
    ps_k = ps_a[0:C, 0, 0:N]
    ps_q = ps_probs[0:C, 1, 512 - N:512]
    ps_v = ps_b[:, 0, 0:PAIRS * C].rearrange("p (w c) -> p w c", c=C)
    ps_proj = ps_b[0:C, 0, 0:N]
    ps_pv = ps_out[:, 0, 0:HP * 4 * VC].rearrange("p (q w e c) -> p q w e c", q=HP, w=2, e=2)
    ps_ot = ps_out[0:C, 0, 384:512]

    normalising_in = sem("normalising_in")
    consts_in = sem("consts_in")
    second_in = sem("second_in")
    rel_in = sem("rel_in")
    set_up = sem("set_up")
    pe_set = sem("pe_set")
    zeroed = sem("zeroed")
    x_landed = [sem("x_landed0"), sem("x_landed1")]
    s = {n: sem(n) for n in (
        "rolled", "centred_ready", "squares_ready", "var_ready", "log_ready", "rstd_ready", "normed_ready",
        "q_ready", "k_ready", "q_copied", "k_copied", "v_ready", "v_copied",
        "scores_ready", "biased", "peak_ready", "shifted", "probs_ready", "turned", "turned_copied",
        "pv_ready", "recip_ready", "heads_ready", "ot_ready", "ot_copied", "proj_ready", "residual_done")}

    FIRST, SECOND = 7, 4
    LEAD = 4

    x = a["x"]
    block = ctx.enter_context(nc.Block())

    @block.sync
    def _(sp):
        def column(name):
            return a[name].rearrange("(c a) -> c a", a=1)

        normalising = ((center[:, :], a["c_center"]), (average[:, :], a["c_average"]))
        first = ((w_in[:, :], a["L0_conv_qkv_w"]),
                 (cols[:, 0:1], column("L0_conv_norm1_g")), (cols[:, 1:2], column("L0_conv_norm1_b")),
                 *((cols[:, 2 + k:3 + k], a["L0_conv_qkv_b"][k * C:(k + 1) * C].rearrange("(c a) -> c a", a=1))
                   for k in range(3)),
                 (head_mask[:, :], a["c_head_mask"]))
        second = ((shift_mask[:, :, :], a["c_shift_mask"]), (ident[:, :], a["c_ident"]),
                  (w_proj[:, :], a["L0_conv_proj_w"]), (cols[:, 5:6], column("L0_conv_proj_b")))
        assert (len(first), len(second)) == (FIRST, SECOND)
        late = weight_loads(a, w_late)

        def step(t, half, par):
            need(sp, s["rolled"], (t - 1) * 3)
            xt = x[bass.ds(t, 1)] if not isinstance(t, int) else x[t:t + 1]
            xt = xt.rearrange("a c h w -> c (a h w)")
            sp.dma_start(x_in[:, par, 0:N - SS * W], xt[:, SS * W:N]).then_inc(x_landed[par], 16)
            sp.dma_start(x_in[:, par, N - SS * W:N], xt[:, 0:SS * W]).then_inc(x_landed[par], 16)

        def after_pair(half):
            if half == 1:
                sp.wait_ge(zeroed_points, 4)
            for dst, src in late[half - 1::LEAD - 1] if half else ():
                sp.dma_start(dst, src).then_inc(weights_in, 16)

        step(0, 0, 0)
        for dst, src in normalising:
            sp.dma_start(dst, src).then_inc(normalising_in, 16)
        for dst, src in first:
            sp.dma_start(dst, src).then_inc(consts_in, 16)
        step(1, 0, 1)
        for dst, src in second:
            sp.dma_start(dst, src).then_inc(second_in, 16)
        table = a["L0_conv_rel_bias"]
        for upper in range(2):
            for y in range(WS):
                runs = bass.AP(table.tensor, y * REL * HEADS, [[HEADS, WS], [REL * HEADS, WS], [1, WS * HEADS]])
                at = upper * WN + y * WS
                sp.dma_start(rel_rows[at:at + WS, :, :].rearrange("p (r c) h -> p r (c h)", r=WS),
                             runs).then_inc(rel_in, 16)
        image_loop(sp, step, lead=LEAD, between=after_pair, start=2)
        sp.wait_ge(weights_in, 16 * len(late))

    @block.gpsimd
    def _(pool):
        nc.gpsimd.memset(w_late["point"][:, :, :], 0.0).then_inc(zeroed_points, 1)
        nc.gpsimd.memset(w_late["taps"][:, :, :], 0.0).then_inc(zeroed_points, 1)
        nc.gpsimd.memset(w_late["point_b"][:, :], 0.0).then_inc(zeroed_points, 1)
        nc.gpsimd.memset(w_late["taps_b"][:, :], 0.0).then_inc(zeroed_points, 1)
        nc.gpsimd.memset(v_blocks[:, :, :, :, :, :, :], 0.0).then_inc(zeroed, 1)
        nc.gpsimd.memset(eps[:, :], EPS).then_inc(zeroed, 1)
        pool.wait_ge(zeroed, 2)
        for e in range(2):
            for par in range(2):
                nc.gpsimd.memset(v_blocks[64 * e:64 * e + 64, par, :, :, :, e, HD:VC], 1.0).then_inc(zeroed, 1)

        def subtract_peak(t, p):
            u = t * 2 + p
            pool.wait_ge(s["peak_ready"], u + 1)
            sc = scores[:, p, :].rearrange("p (h m) -> p h m", m=WN)
            nc.gpsimd.tensor_tensor(sc, sc, peak[:, p, :].unsqueeze(2).to_broadcast((128, HEADS, WN)),
                                    ALU.subtract).then_inc(s["shifted"], 1)

        def step(t, half, par):
            subtract_peak(t, 0)
            subtract_peak(t, 1)

        image_loop(pool, step)

    @block.scalar
    def _(act):
        def square(t):
            act.wait_ge(s["centred_ready"], t + 1)
            need(act, s["var_ready"], t)
            nc.scalar.activation(squares[:, :], centred, ACT.Square).then_inc(s["squares_ready"], 1)

        def inverse_deviation(t):
            act.wait_ge(s["var_ready"], t + 1)
            need(act, s["rstd_ready"], t)
            nc.scalar.activation(log_var[:, :], ps_var, ACT.Ln, bias=eps[:, 0:1]).then_inc(s["log_ready"], 1)
            act.wait_ge(s["log_ready"], t + 1)
            need(act, s["normed_ready"], t)
            nc.scalar.activation(rstd[:, :], log_var[:, :], ACT.Exp, scale=-0.5).then_inc(s["rstd_ready"], 1)

        def copy_q(t):
            if is_image(t, 0):
                act.wait_ge(set_up, 5)
            act.wait_ge(s["q_ready"], t + 1)
            need(act, s["scores_ready"], t * 2)
            nc.scalar.activation(q_sb[:, :], ps_q, ACT.Identity, bias=b_q[:, 0:1], scale=SCALE).then_inc(s["q_copied"], 1)

        def copy_v(t, par):
            act.wait_ge(s["v_ready"], t + 1)
            need(act, s["pv_ready"], (t - 1) * 2)
            for w in range(2):
                for e in range(2):
                    src = ps_v[64 * w:64 * w + 64].rearrange("p a (q e d) -> p a q e d", q=HP, e=2)
                    nc.scalar.copy(v_blocks[64 * e:64 * e + 64, par, :, 0:HP, w, e, 0:HD],
                                   src[:, :, :, e, :]).then_inc(s["v_copied"], 1)

        def exponent(t, p):
            act.wait_ge(s["shifted"], t * 2 + p + 1)
            nc.scalar.activation(scores[:, p, :], scores[:, p, :], ACT.Exp).then_inc(s["probs_ready"], 1)

        def copy_turned(t, p):
            u = t * 2 + p
            for b, cols_b in enumerate((slice(0, 512), slice(512, SC))):
                act.wait_ge(s["turned"], u * 2 + b + 1)
                need(act, s["pv_ready"], u)
                nc.scalar.copy(probs_t[:, cols_b], ps_probs[:, b, 0:cols_b.stop - cols_b.start]).then_inc(s["turned_copied"], 1)

        def copy_ot(t, p, par):
            act.wait_ge(s["ot_ready"], t * 2 + p + 1)
            need(act, s["proj_ready"], t - 1)
            nc.scalar.copy(out_t[:, par, p * 2 * WN:(p + 1) * 2 * WN], ps_ot).then_inc(s["ot_copied"], 1)

        nc.scalar.preload_act_table_set("natural_log_exp_and_others")
        act.wait_ge(zeroed, 6)

        def step(t, half, par):
            if real(t):
                copy_ot(t, 0, par)
            if real(t + 2):
                square(t + 2)
            if real(t):
                copy_turned(t, 1)
            if real(t + 2):
                inverse_deviation(t + 2)
            if real(t + 1):
                exponent(t + 1, 0)
            if real(t + 2):
                copy_q(t + 2)
            if real(t):
                copy_ot(t, 1, par)
            if real(t + 1):
                copy_turned(t + 1, 0)
            if real(t + 2):
                copy_v(t + 2, par)
            if real(t + 1):
                exponent(t + 1, 1)

        led_image_loop(act, step)

    @block.vector
    def _(dve):
        def set_up_rest():
            dve.wait_ge(second_in, 16 * SECOND)
            dve.wait_ge(pe_set, 4)
            nc.vector.tensor_tensor(b_proj[:, :], ps_out[0:C, 0, 0:1], cols[:, 5:6], ALU.add).then_inc(set_up, 1)
            dve.wait_ge(rel_in, 16 * 2 * WS)
            for p in range(PAIRS):
                nc.vector.tensor_tensor(bias[:, p, :].rearrange("p (h m) -> p h m", m=WN),
                                        rel_rows[:, ::-1, :].rearrange("p m h -> p h m"),
                                        shift_mask[:, p, :].unsqueeze(1).to_broadcast((128, HEADS, WN)),
                                        ALU.add).then_inc(set_up, 1)
            dve.wait_ge(set_up, 8)

        def roll(t, half, par):
            dve.wait_ge(x_landed[par], (half + 1) * 32)
            src = grid(x_in[:, par, :])
            dst = windows(stream[:, bass.ds(t * N, N)])
            for w, c0, n, at in ((0, 0, WS, SS), (1, 0, SS, WS + SS), (1, SS, SS, 0)):
                nc.vector.tensor_copy(dst[:, :, w, :, c0:c0 + n],
                                      src[:, :, at:at + n].rearrange("p (a r) c -> p a r c", a=2)).then_inc(s["rolled"], 1)

        def normalise(t):
            dve.wait_ge(s["rstd_ready"], t + 1)
            need(dve, s["v_ready"], t)
            nc.vector.tensor_tensor(normed[:, :], centred, rstd[:, :], ALU.mult).then_inc(s["normed_ready"], 1)

        def copy_k(t):
            dve.wait_ge(s["k_ready"], t + 1)
            need(dve, s["scores_ready"], t * 2)
            nc.vector.scalar_tensor_tensor(out=k_blocks[:, :, :], in0=ps_k.unsqueeze(1).to_broadcast((C, GROUP, N)),
                                           scalar=b_k[:, 0:1],
                                           in1=head_mask[:, :].unsqueeze(2).to_broadcast((C, GROUP, N)),
                                           op0=ALU.add, op1=ALU.mult).then_inc(s["k_copied"], 1)

        def add_bias(t, p):
            u = t * 2 + p
            dve.wait_ge(s["scores_ready"], u + 1)
            need(dve, s["turned"], (u - 1) * 2)
            nc.vector.tensor_tensor(scores[:, p, :].rearrange("p (g c) -> p g c", g=NG),
                                    ps_scores[:, :, 0:GROUP * WN],
                                    bias[:, p, :].rearrange("p (g c) -> p g c", g=NG), ALU.add).then_inc(s["biased"], 1)
            dve.wait_ge(s["biased"], u + 1)
            need(dve, s["shifted"], u - 1)
            nc.vector.tensor_reduce(peak[:, p, :], scores[:, p, :].rearrange("p (h m) -> p h m", m=WN),
                                    AX_X, ALU.max).then_inc(s["peak_ready"], 1)

        def weigh_heads(t, p):
            u = t * 2 + p
            dve.wait_ge(s["pv_ready"], u + 1)
            need(dve, s["heads_ready"], u * 2)
            for w in range(2):
                rows = slice(64 * w, 64 * w + 64)
                nc.vector.reciprocal(recip[rows, :].rearrange("p (q e) -> p q e", e=2),
                                     ps_pv[rows, :, w, :, HD]).then_inc(s["recip_ready"], 1)
            dve.wait_ge(s["recip_ready"], (u + 1) * 2)
            need(dve, s["ot_ready"], u)
            for w in range(2):
                rows = slice(64 * w, 64 * w + 64)
                r = recip[rows, :].rearrange("p (q e) -> p q e", e=2).unsqueeze(3).to_broadcast((64, HP, 2, HD))
                nc.vector.tensor_tensor(heads_out[rows, :].rearrange("p (q e d) -> p q e d", q=HP, e=2),
                                        ps_pv[rows, :, w, :, 0:HD], r, ALU.mult).then_inc(s["heads_ready"], 1)

        def add_residual(t):
            dve.wait_ge(s["proj_ready"], t + 1)
            dst = stream[:, bass.ds(t * N, N)]
            nc.vector.scalar_tensor_tensor(out=dst, in0=ps_proj, scalar=b_proj[:, 0:1], in1=dst,
                                           op0=ALU.add, op1=ALU.add).then_inc(s["residual_done"], 1)

        def step(t, half, par):
            if real(t + 1):
                add_bias(t + 1, 0)
            if real(t - 1):
                add_residual(t - 1)
            if real(t + 3):
                roll(t + 3, half + 1 + par, 1 - par)
            if real(t + 2):
                normalise(t + 2)
            if real(t):
                weigh_heads(t, 1)
            if real(t + 1):
                add_bias(t + 1, 1)
            if real(t + 2):
                copy_k(t + 2)
            if real(t + 1):
                weigh_heads(t + 1, 0)

        roll(0, 0, 0)
        dve.wait_ge(consts_in, 16 * FIRST)
        nc.vector.tensor_scalar(w_qkv[:, :], w_in[:, :], cols[:, 0:1], None, ALU.mult).then_inc(set_up, 1)
        dve.wait_ge(pe_set, 3)
        nc.vector.tensor_tensor(b_q[:, :], ps_out[0:C, 0, 0:1], cols[:, 2:3], ALU.add).then_inc(set_up, 1)
        nc.vector.tensor_tensor(b_k[:, :], ps_out[0:C, 0, 1:2], cols[:, 3:4], ALU.add).then_inc(set_up, 1)
        nc.vector.tensor_tensor(b_v[:, :], ps_out[0:C, 0, 2:3], cols[:, 4:5], ALU.add).then_inc(set_up, 1)
        dve.wait_ge(set_up, 3)
        nc.vector.tensor_scalar(b_q[:, :], b_q[:, :], SCALE, None, ALU.mult).then_inc(set_up, 1)
        led_image_loop(dve, step, tail=2, between=set_up_rest)
        add_residual(B - 1)

    @block.tensor
    def _(pe):
        def fold_q_k_v():
            pe.wait_ge(consts_in, 16 * FIRST)
            for k in range(3):
                nc.tensor.matmul(ps_out[0:C, 0, k:k + 1], w_in[:, k * C:(k + 1) * C], cols[:, 1:2],
                                 start=True, stop=True, skip_group_check=True).then_inc(pe_set, 1)

        def fold_v():
            pe.wait_ge(second_in, 16 * SECOND)
            pe.wait_ge(set_up, 4)
            nc.tensor.matmul(ps_out[0:C, 0, 0:1], w_proj[:, :], b_v[:, 0:1], start=True, stop=True).then_inc(pe_set, 1)
            pe.wait_ge(set_up, 6)

        def centre(t):
            pe.wait_ge(s["rolled"], (t + 1) * 3)
            need(pe, s["k_copied"], t)
            nc.tensor.matmul(centred, center[:, :], stream[:, bass.ds(t * N, N)],
                             start=True, stop=True).then_inc(s["centred_ready"], 1)

        def spread(t):
            pe.wait_ge(s["squares_ready"], t + 1)
            nc.tensor.matmul(ps_var, average[:, :], squares[:, :], start=True, stop=True).then_inc(s["var_ready"], 1)

        def make_q(t):
            if is_image(t, 0):
                pe.wait_ge(set_up, 1)
            pe.wait_ge(s["normed_ready"], t + 1)
            need(pe, s["turned_copied"], (t - 1) * 4)
            nc.tensor.matmul(ps_q, w_qkv[:, 0:C], normed[:, :], start=True, stop=True,
                             skip_group_check=True).then_inc(s["q_ready"], 1)

        def make_k(t):
            pe.wait_ge(s["normed_ready"], t + 1)
            nc.tensor.matmul(ps_k, w_qkv[:, C:2 * C], normed[:, :], start=True, stop=True).then_inc(s["k_ready"], 1)

        def make_v(t):
            pe.wait_ge(s["normed_ready"], t + 1)
            need(pe, s["residual_done"], t - 2)
            for p in range(PAIRS):
                mm = nc.tensor.matmul(ps_v[:, p, :], normed[:, p * 2 * WN:(p + 1) * 2 * WN], w_qkv[:, 2 * C:3 * C],
                                      start=True, stop=True, skip_group_check=True)
            mm.then_inc(s["v_ready"], 1)

        def score(t, p):
            u = t * 2 + p
            pe.wait_ge(s["q_copied"], t + 1)
            pe.wait_ge(s["k_copied"], t + 1)
            need(pe, s["biased"], u)
            for g in range(NG):
                ch = slice(32 * g, 32 * g + 32)
                for w in range(2):
                    tokens = slice((2 * p + w) * WN, (2 * p + w + 1) * WN)
                    q, k = q_sb[ch, tokens], k_blocks[ch, :, tokens]
                    mm = nc.tensor.matmul(ps_scores[64 * w:64 * w + 64, g, 0:GROUP * WN], q, k, start=True, stop=True)
            mm.then_inc(s["scores_ready"], 1)

        def turn(t, p, between=None):
            u = t * 2 + p
            pe.wait_ge(s["probs_ready"], u + 1)
            for b in range(2):
                need(pe, s["turned_copied"], u * 2)
                if b == 1 and between:
                    between()
                if b == 1:
                    pe.wait_ge(s["q_copied"], up_to(t + 1))
                for q in range(b * BANK_HP, min(HP, (b + 1) * BANK_HP)):
                    mm = nc.tensor.transpose(ps_probs[:, b, (q - b * BANK_HP) * 128:(q - b * BANK_HP + 1) * 128],
                                             scores[:, p, q * 128:(q + 1) * 128], ident[:, :])
                mm.then_inc(s["turned"], 1)

        def weigh(t, p, par):
            u = t * 2 + p
            pe.wait_ge(s["v_copied"], (t + 1) * 4)
            need(pe, s["ot_copied"], u)
            for q in range(HP):
                if q % BANK_HP == 0:
                    pe.wait_ge(s["turned_copied"], u * 2 + q // BANK_HP + 1)
                mm = nc.tensor.matmul(ps_out[:, 0, q * 4 * VC:(q + 3) * 4 * VC], probs_t[:, q * 128:(q + 1) * 128],
                                      v_blocks[:, par, p, q:q + 3, :, :, :].rearrange("p q w e c -> p (q w e c)"),
                                      start=True, stop=True, skip_group_check=True)
            mm.then_inc(s["pv_ready"], 1)

        def turn_heads(t, p):
            u = t * 2 + p
            pe.wait_ge(s["heads_ready"], (u + 1) * 2)
            nc.tensor.transpose(ps_ot, heads_out[:, :], ident[:, :]).then_inc(s["ot_ready"], 1)

        def project(t, par):
            pe.wait_ge(s["ot_copied"], (t + 1) * 2)
            pe.wait_ge(s["v_copied"], up_to(t + 2) * 4)
            nc.tensor.matmul(ps_proj, w_proj[:, :], out_t[:, par, :], start=True, stop=True).then_inc(s["proj_ready"], 1)

        def step(t, half, par):
            if real(t):
                turn_heads(t, 0)
            if real(t + 2):
                centre(t + 2)
            if is_image(t, -2):
                fold_q_k_v()
            if real(t):
                turn(t, 1)
            if real(t + 2):
                spread(t + 2)
            if real(t):
                weigh(t, 1, par)
            if real(t + 1):
                score(t + 1, 1)
            if real(t + 2):
                make_q(t + 2)
            if real(t):
                turn_heads(t, 1)
            if real(t + 1):
                turn(t + 1, 0, between=(lambda: make_k(t + 2)) if real(t + 2) else None)
            elif real(t + 2):
                make_k(t + 2)
            if real(t + 2):
                make_v(t + 2)
            if real(t + 1):
                weigh(t + 1, 0, 1 - par)
            if real(t):
                project(t, par)
            if real(t + 2):
                score(t + 2, 0)

        pe.wait_ge(normalising_in, 16 * 2)
        led_image_loop(pe, step, between=fold_v)


def chunk_loop(engine, n, step):
    step(0, 0, 0)
    step(1, 0, 1)
    with engine.Fori(1, n // 2 - 1) as i:
        step(i * 2, i, 0)
        step(i * 2 + 1, i, 1)
    step(n - 2, n // 2 - 1, 0)
    step(n - 1, n // 2 - 1, 1)


def mlp(nc, ctx, sem, stream, mixed, stats, center, average, w):
    CHUNKS = B * N // CHUNK
    QUARTERS = 4

    def sb(name, shape, dt=F32):
        return ctx.enter_context(nc.sbuf_tensor(name, shape, dt))

    fc1 = sb("fc1_scaled", [C, HID])
    fc1_b = sb("fc1_b_folded", [128, HT])
    squares = sb("squares2", [C, 2, CHUNK])
    log_var = sb("log_var2", [C, 2, CHUNK])
    rstd = sb("rstd2", [C, 2, CHUNK])
    eps = sb("eps2", [C, 1])
    summed = sb("summed", [C, 2, CHUNK])
    hidden = sb("hidden", [128, 2, HT, CHUNK])
    ps_hidden = ctx.enter_context(nc.psum_tensor("ps_hidden", [128, 2 * HT, CHUNK], F32))
    ps_y = ctx.enter_context(nc.psum_tensor("ps_y", [128, 2, CHUNK], F32))
    ps_centred = ps_y[0:C, :, :]
    ps_var = ps_hidden[:, 2 * HT - 2:2 * HT, :]

    eps_set = sem("eps_set")
    set_up = sem("set_up_mlp")
    pe_set = sem("pe_set_mlp")
    s = {n: sem(n + "_2") for n in (
        "centred_ready", "squares_ready", "centred_copied", "var_ready", "log_ready", "rstd_ready", "normed_ready",
        "hidden_ready", "gelu_ready", "y_ready", "sum_ready", "mixed_ready", "stats_ready")}
    block = ctx.enter_context(nc.Block())

    @block.gpsimd
    def _(pool):
        nc.gpsimd.memset(eps[:, :], EPS).then_inc(eps_set, 1)

    @block.tensor
    def _(pe):
        def centre(k, par):
            need(pe, s["centred_copied"], k - 1)
            nc.tensor.matmul(ps_centred[:, par, :], center[:, :], stream[:, bass.ds(k * CHUNK, CHUNK)],
                             start=True, stop=True).then_inc(s["centred_ready"], 1)

        def spread(k, par):
            pe.wait_ge(s["squares_ready"], k + 1)
            need(pe, s["log_ready"], k - 1)
            nc.tensor.matmul(ps_var[0:C, par, :], average[:, :], squares[:, par, :],
                             start=True, stop=True).then_inc(s["var_ready"], 1)

        def normalise_step(k, half, par):
            if not is_image(k, CHUNKS - 1):
                centre(k + 1, 1 - par)
            spread(k, par)

        centre(0, 0)
        for h in range(HT):
            nc.tensor.matmul(ps_var[:, 1, h:h + 1], w["fc1"][:, h * 128:(h + 1) * 128], w["norm2_b"][:, :],
                             start=True, stop=True, skip_group_check=True).then_inc(pe_set, 1)
        pe.wait_ge(set_up, 2)
        chunk_loop(pe, CHUNKS, normalise_step)

        def up(k, par):
            need(pe, s["gelu_ready"], (k - 1) * HT)
            for h in range(HT):
                nc.tensor.matmul(ps_hidden[:, par * HT + h, :], fc1[:, h * 128:(h + 1) * 128],
                                 mixed[:, bass.ds(k * CHUNK, CHUNK)], start=True, stop=True).then_inc(s["hidden_ready"], 1)

        def down(k, par):
            need(pe, s["sum_ready"], k - 1)
            for h in range(HT):
                pe.wait_ge(s["gelu_ready"], k * HT + h + 1)
                mm = nc.tensor.matmul(ps_y[0:C, par, :], w["fc2"][:, h, :], hidden[:, par, h, :],
                                      start=(h == 0), stop=(h == HT - 1))
            mm.then_inc(s["y_ready"], 1)

        def step(k, half, par):
            if not is_image(k, CHUNKS - 1):
                up(k + 1, 1 - par)
            down(k, par)

        pe.wait_ge(s["normed_ready"], 1)
        up(0, 0)
        pe.wait_ge(s["normed_ready"], CHUNKS)
        chunk_loop(pe, CHUNKS, step)

    @block.scalar
    def _(act):
        def square(k, par):
            act.wait_ge(s["centred_ready"], k + 1)
            need(act, s["var_ready"], k - 1)
            nc.scalar.activation(squares[:, par, :], ps_centred[:, par, :], ACT.Square).then_inc(s["squares_ready"], 1)

        def normalise_step(k, half, par):
            if not is_image(k, CHUNKS - 1):
                square(k + 1, 1 - par)
            act.wait_ge(s["var_ready"], k + 1)
            need(act, s["rstd_ready"], k - 1)
            nc.scalar.activation(log_var[:, par, :], ps_var[0:C, par, :], ACT.Ln, bias=eps[:, 0:1]).then_inc(s["log_ready"], 1)
            act.wait_ge(s["log_ready"], k + 1)
            need(act, s["normed_ready"], k - 1)
            nc.scalar.activation(rstd[:, par, :], log_var[:, par, :], ACT.Exp, scale=-0.5).then_inc(s["rstd_ready"], 1)

        nc.scalar.preload_act_table_set("natural_log_exp_and_others")
        act.wait_ge(eps_set, 1)
        square(0, 0)
        chunk_loop(act, CHUNKS, normalise_step)

        def step(k, half, par):
            need(act, s["y_ready"], k - 1)
            for h in range(HT):
                act.wait_ge(s["hidden_ready"], k * HT + h + 1)
                nc.scalar.activation(hidden[:, par, h, :], ps_hidden[:, par * HT + h, :], ACT.Gelu,
                                     bias=fc1_b[:, h:h + 1]).then_inc(s["gelu_ready"], 1)

        nc.scalar.preload_act_table_set("gelu_and_others")
        chunk_loop(act, CHUNKS, step)

    @block.vector
    def _(dve):
        nc.vector.tensor_scalar(fc1[:, :], w["fc1"][:, :], w["norm2_g"][:, 0:1], None, ALU.mult).then_inc(set_up, 1)
        dve.wait_ge(pe_set, HT)
        nc.vector.tensor_tensor(fc1_b[:, :], ps_var[:, 1, 0:HT], w["fc1_b"][:, :], ALU.add).then_inc(set_up, 1)

        def copy_centred(k, par):
            dve.wait_ge(s["squares_ready"], k + 1)
            nc.vector.tensor_copy(mixed[:, bass.ds(k * CHUNK, CHUNK)], ps_centred[:, par, :]).then_inc(s["centred_copied"], 1)

        def normalise_step(k, half, par):
            if not is_image(k, CHUNKS - 1):
                copy_centred(k + 1, 1 - par)
            dve.wait_ge(s["rstd_ready"], k + 1)
            dve.wait_ge(s["centred_copied"], k + 1)
            chunk = mixed[:, bass.ds(k * CHUNK, CHUNK)]
            nc.vector.tensor_tensor(chunk, chunk, rstd[:, par, :], ALU.mult).then_inc(s["normed_ready"], 1)

        copy_centred(0, 0)
        chunk_loop(dve, CHUNKS, normalise_step)

        def step(k, half, par):
            dve.wait_ge(s["y_ready"], k + 1)
            need(dve, s["mixed_ready"], (k - 1) * 2 * QUARTERS)
            nc.vector.scalar_tensor_tensor(out=summed[:, par, :], in0=ps_y[0:C, par, :], scalar=w["fc2_b"][:, 0:1],
                                           in1=stream[:, bass.ds(k * CHUNK, CHUNK)],
                                           op0=ALU.add, op1=ALU.add).then_inc(s["sum_ready"], 1)
            dve.wait_ge(s["sum_ready"], k + 1)
            for j in range(2):
                src = windows(summed[:, par, j * N:(j + 1) * N])
                dst = mixed[:, bass.ds(k * CHUNK + j * N, N)].rearrange("p (a r b c) -> p a r b c", a=4, r=SS, b=4)
                blocks, order = (slice(1, 4, 2), slice(0, 3, 2)), (slice(None), slice(None, None, -1))
                for top in range(2):
                    for left in range(2):
                        rows, cs = slice(top * SS, top * SS + SS), slice(left * SS, left * SS + SS)
                        nc.vector.tensor_copy(
                            dst[:, blocks[top], :, blocks[left], :].rearrange("p a r b c -> p a b r c"),
                            src[:, order[top], order[left], rows, cs]).then_inc(s["mixed_ready"], 1)
            for j in range(2):
                dve.wait_ge(s["mixed_ready"], k * 2 * QUARTERS + (j + 1) * QUARTERS)
                nc.vector.bn_stats(stats[:, bass.ds(k * 2 + j, 1), :], mixed[:, bass.ds(k * CHUNK + j * N, N)]).then_inc(s["stats_ready"], 1)

        chunk_loop(dve, CHUNKS, step)


def channel_attention(nc, ctx, sem, v_sb, mixed, stats, ident, average, w, stack_ones, out):
    def sb(name, shape, dt=F32):
        return ctx.enter_context(nc.sbuf_tensor(name, shape, dt))

    def bank(name, count=1):
        return ctx.enter_context(nc.psum_tensor(name, [128, count, 512], F32))

    moments = sb("moments", [C, B, 2])
    mean2 = sb("mean2", [C, B, 2])
    mean = sb("mean", [C, B])
    spread2 = sb("spread2", [C, B, 2])
    log_var = sb("log_var3", [C, B])
    eps = sb("eps3", [C, 1])
    products = sb("products", [3 * SET, SETS, SIDE, STACK])
    conv_w = sb("conv_w", [STACK, SETS, SIDE, 3 * SET])
    final_w = sb("final_w", [C, C])
    recip_alpha = sb("recip_alpha", [C, 1])
    moment = sb("moment", [C, 2])
    x_scaled = sb("x_scaled", [C, N])
    x_gained = sb("x_gained", [C, N])
    x_pad = sb("x_pad", [SETS * SET, 2, PADW, PADW])
    x_stack = sb("x_stack", [STACK, 2, SETS, ROWS])
    qkv = sb("qkv", [3 * SET, 2, SETS, N])
    tokens = sb("tokens", [128, 2, 2, SETS * SET])
    logits = sb("logits", [C, C])
    peak = sb("peak3", [C, 1])
    neg_peak = sb("neg_peak", [C, 1])
    row_sum = sb("row_sum", [C, 1])
    recip_sum = sb("recip_sum", [C, 1])
    attn = sb("attn", [C, C])
    av_sb = sb("av_sb", [C, N])
    y_sb = sb("y_sb", [C, 2, N])
    padded_x = nc.dram_tensor("padded_x", (B, SETS * SET, PADW * PADW), F32, kind="Internal").ap()

    ps_qkv = bank("ps_qkv", SETS)
    ps_tok_bank = bank("ps_tok")
    ps_tok = ps_tok_bank[:, 0, 0:2 * SETS * 2 * SET].rearrange("p (n s c) -> p n s c", n=2, s=SETS)
    ps_gram = bank("ps_gram")[0:C, 0, 0:C]
    ps_av = bank("ps_av")[0:C, 0, 0:N]
    ps_y_bank = bank("ps_y3")
    ps_y = ps_y_bank[0:C, 0, 0:N]
    ps_moments = ps_y_bank[0:C, 0, 0:2 * B]

    zeroed = sem("zeroed3")
    ones_in = sem("ones_in")
    moments_set = sem("moments_set")
    moments_pe = sem("moments_pe")
    log_set = sem("log_set")
    rstd_set = sem("rstd_set")
    products_set = sem("products_set")
    weights_turned = sem("weights_turned")
    weights_copied = sem("weights_copied")
    alpha_set = sem("alpha_set")
    written = [sem("written0"), sem("written1")]
    stacked = [sem("stacked0"), sem("stacked1")]
    v_moved = [sem("v_moved0"), sem("v_moved1")]
    out_done = [sem("out_done0"), sem("out_done1")]
    s = {n: sem(n + "_3") for n in (
        "moment_ready", "scaled", "gained", "normed", "x_padded", "conv_ready", "evacuated", "tok_ready",
        "tok_copied", "gram_ready", "logits_ready", "peak_ready", "neg_ready", "exp_ready", "recip_ready",
        "attn_ready", "av_ready", "av_copied", "final_ready", "y_ready")}
    SHIFT_LOADS, MOVES = SIDE, SETS

    def pads_zeroed(engine):
        engine.wait_ge(zeroed, 3)

    block = ctx.enter_context(nc.Block())

    @block.sync
    def _(sp):
        sp.dma_start(x_stack[SIDE * SET:STACK, :, :, :], stack_ones).then_inc(ones_in, 16)
        pads_zeroed(sp)

        def write(t, par):
            pads_zeroed(sp)
            sp.wait_ge(s["x_padded"], t + 1)
            sp.dma_start(padded_x[bass.ds(t, 1)].rearrange("a p m -> (a p) m"), x_pad[:, par, :, :].rearrange("p r c -> p (r c)")).then_inc(written[par], 16)

        def stack(t, half, par):
            pads_zeroed(sp)
            sp.wait_ge(written[par], (half + 1) * 16)
            need(sp, s["conv_ready"], (t - 1) * SETS)
            for i in range(SIDE):
                sp.dma_start(x_stack[i * SET:(i + 1) * SET, par, :, :],
                             padded_x[bass.ds(t, 1), :, i * PADW:i * PADW + ROWS].rearrange("a (s c) m -> (a c) s m", c=SET)
                             ).then_inc(stacked[par], 16)

        def store(t, par):
            pads_zeroed(sp)
            sp.wait_ge(s["y_ready"], t + 1)
            sp.dma_start(out[bass.ds(t, 1)].rearrange("a c h w -> c (a h w)"), y_sb[:, par, :]).then_inc(out_done[par], 16)

        write(0, 0)
        stack(0, 0, 0)
        write(1, 1)
        stack(1, 0, 1)
        write(2, 0)
        write(3, 1)

        def step(t, half, par):
            if not past(t + 2):
                stack(t + 2, half + 1, par)
            if not past(t + 4):
                write(t + 4, par)
            if not is_image(t, 0):
                store(t - 1, 1 - par)

        image_loop(sp, step, tail=3)
        store(B - 1, 1)
        for par in range(2):
            sp.wait_ge(out_done[par], 16 * (B // 2))

    @block.gpsimd
    def _(pool):
        nc.gpsimd.memset(products[:, :, :, :], 0.0).then_inc(zeroed, 1)
        nc.gpsimd.memset(eps[:, :], EPS).then_inc(zeroed, 1)
        nc.gpsimd.memset(x_pad[:, :, :, :], 0.0).then_inc(zeroed, 1)

        def move_v(t, par):
            pads_zeroed(pool)
            pool.wait_ge(s["evacuated"], (t + 1) * SETS)
            for g in range(SETS):
                count = min(SET, C - g * SET)
                pool.dma_start(v_sb[g * SET:g * SET + count, bass.ds(t * N, N)],
                              qkv[2 * SET:2 * SET + count, par, g, :]).then_inc(v_moved[par], 16)

        def step(t, half, par):
            move_v(t, par)

        image_loop(pool, step)

    @block.scalar
    def _(act):
        nc.scalar.preload_act_table_set("natural_log_exp_and_others")
        pads_zeroed(act)
        act.wait_ge(moments_set, 7)
        nc.scalar.activation(log_var[:, :], spread2[:, :, 0], ACT.Ln, scale=0.5, bias=eps[:, 0:1]).then_inc(log_set, 1)
        act.wait_ge(log_set, 1)
        nc.scalar.activation(moments[:, :, 0], log_var[:, :], ACT.Exp, scale=-0.5).then_inc(rstd_set, 1)
        act.wait_ge(moments_set, 8)

        def scale(t):
            pads_zeroed(act)
            need(act, s["scaled"], t)
            nc.scalar.copy(moment[:, :], moments[:, bass.ds(t, 1), :].rearrange("p a b -> p (a b)")).then_inc(s["moment_ready"], 1)
            pads_zeroed(act)
            act.wait_ge(s["moment_ready"], t + 1)
            need(act, s["gained"], t)
            nc.scalar.activation(x_scaled[:, :], mixed[:, bass.ds(t * N, N)], ACT.Identity, bias=moment[:, 1:2],
                                 scale=moment[:, 0:1]).then_inc(s["scaled"], 1)

        def pad_x(t, par):
            pads_zeroed(act)
            act.wait_ge(s["normed"], t + 1)
            nc.scalar.copy(x_pad[0:C, par, 1:H + 1, 1:W + 1], grid(mixed[:, bass.ds(t * N, N)])).then_inc(s["x_padded"], 1)

        def evacuate(t, half, par, g):
            act.wait_ge(s["conv_ready"], t * SETS + g + 1)
            need(act, s["tok_ready"], t - 1)
            need(act, v_moved[par], half * 16 * MOVES)
            nc.scalar.copy(qkv[:, par, g, :], ps_qkv[0:3 * SET, g, 0:N]).then_inc(s["evacuated"], 1)

        def exponent(t):
            act.wait_ge(s["neg_ready"], t + 1)
            need(act, s["recip_ready"], t)
            nc.scalar.activation(logits[:, :], logits[:, :], ACT.Exp, bias=neg_peak[:, 0:1],
                                 accum_out=row_sum[:, 0:1]).then_inc(s["exp_ready"], 1)

        def copy_av(t):
            act.wait_ge(s["av_ready"], t + 1)
            need(act, s["final_ready"], t)
            nc.scalar.copy(av_sb[:, :], ps_av).then_inc(s["av_copied"], 1)

        scale(0)
        pad_x(0, 0)
        scale(1)
        pad_x(1, 1)
        for g in range(SETS):
            act.wait_ge(weights_turned, SIDE * (g + 1))
            nc.scalar.copy(conv_w[:, g, :, :], ps_qkv[0:STACK, g, 0:SIDE * 3 * SET].rearrange("p (j m) -> p j m", j=SIDE)).then_inc(weights_copied, 1)
        act.wait_ge(weights_turned, SIDE * SETS + 1)
        nc.scalar.copy(final_w[:, :], ps_gram).then_inc(weights_copied, 1)
        scale(2)
        pad_x(2, 0)
        scale(3)
        pad_x(3, 1)
        scale(4)
        for g in range(SETS):
            evacuate(0, 0, 0, g)

        def step(t, half, par):
            if not is_image(t, 0):
                copy_av(t - 1)
            if not past(t + 1):
                evacuate(t + 1, half + par, 1 - par, 0)
            exponent(t)
            if not past(t + 1):
                evacuate(t + 1, half + par, 1 - par, 1)
                evacuate(t + 1, half + par, 1 - par, 2)
            if not past(t + 5):
                scale(t + 5)
            if not past(t + 4):
                pad_x(t + 4, par)

        image_loop(act, step, tail=3)
        copy_av(B - 1)

    @block.vector
    def _(dve):
        means, deviations = stats[:, :, 1::3], stats[:, :, 2::3]
        dve.wait_ge(moments_pe, 1)
        nc.vector.tensor_copy(mean2[:, :, :], ps_moments.rearrange("p (t e) -> p t e", e=2)).then_inc(moments_set, 1)
        dve.wait_ge(moments_set, 1)
        nc.vector.tensor_tensor(mean[:, :], mean2[:, :, 0], mean2[:, :, 1], ALU.add).then_inc(moments_set, 1)
        dve.wait_ge(moments_set, 2)
        nc.vector.tensor_scalar(mean[:, :], mean[:, :], 0.5, None, ALU.mult).then_inc(moments_set, 1)
        dve.wait_ge(moments_set, 3)
        nc.vector.tensor_tensor(mean2[:, :, :], means, mean[:, :].unsqueeze(2).to_broadcast((C, B, 2)),
                                ALU.subtract).then_inc(moments_set, 1)
        dve.wait_ge(moments_set, 4)
        nc.vector.tensor_tensor(spread2[:, :, :], mean2[:, :, :], mean2[:, :, :], ALU.mult).then_inc(moments_set, 1)
        dve.wait_ge(moments_set, 5)
        nc.vector.scalar_tensor_tensor(out=spread2[:, :, :], in0=deviations, scalar=2.0 / N, in1=spread2[:, :, :],
                                       op0=ALU.mult, op1=ALU.add).then_inc(moments_set, 1)
        dve.wait_ge(moments_pe, 2)
        nc.vector.tensor_reduce(spread2[:, :, 0], ps_moments.rearrange("p (t e) -> p t e", e=2), AX_X,
                                ALU.add).then_inc(moments_set, 1)
        dve.wait_ge(rstd_set, 1)
        nc.vector.scalar_tensor_tensor(out=moments[:, :, 1], in0=mean[:, :], scalar=-1.0, in1=moments[:, :, 0],
                                       op0=ALU.mult, op1=ALU.mult).then_inc(moments_set, 1)

        def affine(t, half, par):
            dve.wait_ge(s["scaled"], t + 1)
            need(dve, s["normed"], t)
            nc.vector.tensor_tensor(x_gained[:, :], x_scaled[:, :], w["ln_g"][:, :], ALU.mult).then_inc(s["gained"], 1)
            dve.wait_ge(s["gained"], t + 1)
            need(dve, written[par], half * 16)
            nc.vector.tensor_tensor(mixed[:, bass.ds(t * N, N)], x_gained[:, :], w["ln_b"][:, :],
                                    ALU.add).then_inc(s["normed"], 1)

        def copy_tokens(t):
            dve.wait_ge(s["tok_ready"], t + 1)
            need(dve, s["gram_ready"], t)
            for n in range(2):
                nc.vector.tensor_copy(tokens[:, n, :, :].rearrange("p k (s c) -> p s k c", s=SETS),
                                      ps_tok[:, n, :, :].rearrange("p s (k c) -> p s k c", k=2)).then_inc(s["tok_copied"], 1)

        def make_logits(t):
            dve.wait_ge(s["gram_ready"], t + 1)
            need(dve, s["attn_ready"], t)
            nc.vector.scalar_tensor_tensor(out=logits[:, :], in0=ps_gram, scalar=recip_alpha[:, 0:1],
                                           in1=w["block_mask"][:, :], op0=ALU.mult, op1=ALU.add).then_inc(s["logits_ready"], 1)
            dve.wait_ge(s["logits_ready"], t + 1)
            need(dve, s["neg_ready"], t)
            nc.vector.tensor_reduce(peak[:, :], logits[:, :], AX_X, ALU.max).then_inc(s["peak_ready"], 1)
            dve.wait_ge(s["peak_ready"], t + 1)
            need(dve, s["exp_ready"], t)
            nc.vector.tensor_scalar(neg_peak[:, :], peak[:, :], -1.0, None, ALU.mult).then_inc(s["neg_ready"], 1)

        def normalise(t):
            dve.wait_ge(s["exp_ready"], t + 1)
            nc.vector.reciprocal(recip_sum[:, :], row_sum[:, :]).then_inc(s["recip_ready"], 1)
            dve.wait_ge(s["recip_ready"], t + 1)
            need(dve, s["av_ready"], t)
            nc.vector.tensor_scalar(attn[:, :], logits[:, :], recip_sum[:, 0:1], None, ALU.mult).then_inc(s["attn_ready"], 1)

        def finish(t, half, par):
            dve.wait_ge(s["final_ready"], t + 1)
            need(dve, out_done[par], half * 16)
            nc.vector.scalar_tensor_tensor(out=y_sb[:, par, :], in0=ps_y, scalar=w["final_b"][:, 0:1],
                                           in1=mixed[:, bass.ds(t * N, N)], op0=ALU.add, op1=ALU.add).then_inc(s["y_ready"], 1)

        affine(0, 0, 0)
        dve.wait_ge(zeroed, 3)
        for g in range(SETS):
            taps = w["taps"][:, g, :].rearrange("p (i j) -> p j i", i=SIDE)
            nc.vector.tensor_tensor(products[:, g, :, 0:SIDE * SET].rearrange("p j (i c) -> p j i c", i=SIDE),
                                    w["point"][:, g, :].unsqueeze(1).unsqueeze(1).to_broadcast((3 * SET, SIDE, SIDE, SET)),
                                    taps.unsqueeze(3).to_broadcast((3 * SET, SIDE, SIDE, SET)),
                                    ALU.mult).then_inc(products_set, 1)
            nc.vector.tensor_scalar(products[:, g, :, SIDE * SET:SIDE * SET + SIDE], taps, w["point_b"][:, g:g + 1], None,
                                    ALU.mult).then_inc(products_set, 1)
            nc.vector.tensor_copy(products[:, g, 0, STACK - 1:STACK], w["taps_b"][:, g:g + 1]).then_inc(products_set, 1)
        affine(1, 0, 1)
        nc.vector.reciprocal(recip_alpha[:, :], w["alpha"][:, :]).then_inc(alpha_set, 1)
        affine(2, 1, 0)
        affine(3, 1, 1)
        dve.wait_ge(alpha_set, 1)

        def step(t, half, par):
            copy_tokens(t)
            make_logits(t)
            normalise(t)
            if not past(t + 4):
                affine(t + 4, half + 2, par)
            if not is_image(t, 0):
                finish(t - 1, half if par else half - 1, 1 - par)

        image_loop(dve, step, tail=3)
        finish(B - 1, B // 2 - 1, 1)

    @block.tensor
    def _(pe):
        nc.tensor.matmul(ps_moments, average[:, :], stats[:, :, 1::3], start=True, stop=True).then_inc(moments_pe, 1)
        pe.wait_ge(moments_set, 6)
        nc.tensor.matmul(ps_moments, average[:, :], spread2[:, :, :], start=True, stop=True).then_inc(moments_pe, 1)
        for g in range(SETS):
            pe.wait_ge(products_set, 3 * (g + 1))
            for j in range(SIDE):
                nc.tensor.transpose(ps_qkv[0:STACK, g, j * 3 * SET:(j + 1) * 3 * SET], products[:, g, j, :],
                                    ident[0:3 * SET, 0:3 * SET]).then_inc(weights_turned, 1)
        nc.tensor.transpose(ps_gram, w["final"][:, :], ident[0:C, 0:C]).then_inc(weights_turned, 1)
        pe.wait_ge(weights_copied, SETS + 1)
        pe.wait_ge(ones_in, 16)

        def convolve(t, half, par, g):
            pe.wait_ge(stacked[par], (half + 1) * 16 * SHIFT_LOADS)
            need(pe, s["evacuated"], (t - 1) * SETS + g + 1)
            for j in range(SIDE):
                mm = nc.tensor.matmul(ps_qkv[0:3 * SET, g, 0:N], conv_w[:, g, j, :],
                                      grid(x_stack[:, par, g, :], PADW)[:, :, j:j + W],
                                      start=(j == 0), stop=(j == SIDE - 1))
            mm.then_inc(s["conv_ready"], 1)

        def turn_tokens(t, par):
            need(pe, s["tok_copied"], t * 2)
            for g in range(SETS):
                pe.wait_ge(s["evacuated"], t * SETS + g + 1)
                for n in range(2):
                    mm = nc.tensor.transpose(ps_tok[:, n, g, :], qkv[0:2 * SET, par, g, n * 128:(n + 1) * 128],
                                             ident[0:2 * SET, 0:2 * SET])
            mm.then_inc(s["tok_ready"], 1)

        def gram(t):
            pe.wait_ge(s["tok_copied"], (t + 1) * 2)
            need(pe, s["logits_ready"], t)
            for n in range(2):
                mm = nc.tensor.matmul(ps_gram, tokens[:, n, 1, 0:C], tokens[:, n, 0, 0:C], start=(n == 0), stop=(n == 1))
            mm.then_inc(s["gram_ready"], 1)

        def attend(t, half, par):
            pe.wait_ge(s["attn_ready"], t + 1)
            pe.wait_ge(v_moved[par], (half + 1) * 16 * MOVES)
            need(pe, s["av_copied"], t)
            nc.tensor.matmul(ps_av, attn[:, :], v_sb[:, bass.ds(t * N, N)], start=True, stop=True).then_inc(s["av_ready"], 1)

        def finalise(t):
            pe.wait_ge(s["av_copied"], t + 1)
            need(pe, s["y_ready"], t)
            nc.tensor.matmul(ps_y, final_w[:, :], av_sb[:, :], start=True, stop=True).then_inc(s["final_ready"], 1)

        for g in range(SETS):
            convolve(0, 0, 0, g)

        def step(t, half, par):
            turn_tokens(t, par)
            if not is_image(t, 0):
                attend(t - 1, half if par else half - 1, 1 - par)
            if not past(t + 1):
                convolve(t + 1, half + par, 1 - par, 0)
            gram(t)
            if not past(t + 1):
                convolve(t + 1, half + par, 1 - par, 1)
                convolve(t + 1, half + par, 1 - par, 2)
            if not is_image(t, 0):
                finalise(t - 1)

        image_loop(pe, step, tail=3)
        attend(B - 1, B // 2 - 1, 1)
        finalise(B - 1)


_INS = ['x', 'L0_conv_qkv_w', 'L0_conv_qkv_b', 'L0_conv_proj_w', 'L0_conv_proj_b', 'L0_conv_rel_bias',
        'L0_conv_norm1_g', 'L0_conv_norm1_b', 'L0_conv_norm2_g', 'L0_conv_norm2_b', 'L0_conv_fc1_w',
        'L0_conv_fc1_b', 'L0_conv_fc2_w', 'L0_conv_fc2_b', 'L1_conv_ln_g', 'L1_conv_ln_b', 'L1_conv_wq_p',
        'L1_conv_bq_p', 'L1_conv_wq_d', 'L1_conv_bq_d', 'L1_conv_wk_p', 'L1_conv_bk_p', 'L1_conv_wk_d',
        'L1_conv_bk_d', 'L1_conv_wv_p', 'L1_conv_bv_p', 'L1_conv_wv_d', 'L1_conv_bv_d', 'L1_conv_alpha',
        'L1_conv_w_f', 'L1_conv_b_f']


def constants():
    f = np.float32
    head_mask = np.zeros((C, GROUP), f)
    for c in range(C):
        head_mask[c, (c // HD) % GROUP] = 1
    region = np.repeat([0, 1, 2], [H - WS, WS - SS, SS])
    label = region[:, None] * 3 + region[None, :]
    shift = np.zeros((2, WN, PAIRS, WN), f)
    for p in range(PAIRS):
        for w in range(2):
            win = label[p * WS:(p + 1) * WS, w * WS:(w + 1) * WS].reshape(-1)
            shift[w, :, p, :] = np.where(win[:, None] != win[None, :], -10.0, 0.0)
    head = np.arange(C) // HC
    ones = np.pad(np.ones((H, W), f), 1).reshape(-1)
    stack = np.stack([ones[i * PADW:i * PADW + ROWS] for i in range(SIDE)] + [np.ones(ROWS, f)])
    return {
        "c_stack_ones": np.ascontiguousarray(np.broadcast_to(stack[:, None, None], (SIDE + 1, 2, SETS, ROWS))),
        "c_ident": np.eye(128, dtype=f),
        "c_center": (np.eye(C) - 1.0 / C).astype(f),
        "c_average": np.full((C, C), 1.0 / C, f),
        "c_head_mask": head_mask,
        "c_shift_mask": shift.reshape(128, PAIRS, WN),
        "c_block_mask": np.where(head[:, None] == head[None, :], 0.0, BLOCKED).astype(f),
    }


def kernel(**inputs):
    import concourse.bacc as _bacc
    from concourse.bass_utils import run_bass_kernel_spmd as _run

    nc = _bacc.Bacc("TRN2", target_bir_lowering=False, num_devices=1)
    arrays, args = {}, {}
    given = {name: np.ascontiguousarray(inputs[name]) for name in _INS}
    for name, v in {**given, **constants()}.items():
        arrays[f"in_{name}"] = v
        args[name] = nc.dram_tensor(f"in_{name}", v.shape, mybir.dt.from_np(v.dtype), kind="ExternalInput").ap()
    args["out"] = nc.dram_tensor("out_0", (B, C, H, W), F32, kind="ExternalOutput").ap()
    build(nc, args)
    r = _run(nc, [arrays], core_ids=[0])
    return r.results[0]["out_0"]
```
